# Optimizing a Trainium2 kernel written in Bass

```python
import numpy as np
import jax
import jax.numpy as jnp

def _softmax(x, axis=-1):
    return jax.nn.softmax(x, axis=axis)

def _gelu(x):
    return jax.nn.gelu(x, approximate=True)

def _silu(x):
    return jax.nn.silu(x)

def _sigmoid(x):
    return jax.nn.sigmoid(x)

def _layernorm(x, axis=-1, eps=1e-05):
    m = jnp.mean(x, axis=axis, keepdims=True)
    v = jnp.var(x, axis=axis, keepdims=True)
    return (x - m) / jnp.sqrt(v + eps)

def _scatter_add(tgt, idx, src, axis=0):
    return tgt.at[idx].add(src)

def _segment_sum(src, seg, n):
    return jax.ops.segment_sum(src, seg, n)
kernel_name = 'mk_prb_d1_jaxref_r8_fab4a4'

def setup_inputs(seed: int=0):
    np.random.seed(seed)
    _w = jnp.asarray

    def _L0_attn_setup():
        import jax, jax.numpy as jnp
        import numpy as np
        EPS = 1e-08
        GROUPS = 128

        def log_g(x):
            return jnp.where(x >= 0, jnp.log(jax.nn.relu(x) + 0.5 + EPS), -jax.nn.softplus(-x) + EPS)

        def grouped_linear(x, W):
            B, S, D = x.shape
            G = W.shape[0]
            xg = x.reshape(B, S, G, D // G)
            y = jnp.einsum('bsgi,goi->bsgo', xg, W)
            return y.reshape(B, S, -1)

        def parallel_scan_log(log_coeffs, log_values):
            a_star = jnp.cumsum(log_coeffs + EPS, axis=1)
            log_h0_plus_b_star = jax.lax.cumlogsumexp(log_values - a_star, axis=1)
            return jnp.exp(a_star + log_h0_plus_b_star)
        key = jax.random.key(seed)
        k_x, k_f, k_i, k_h = jax.random.split(key, 4)
        B, S, D, H = (4, 1024, 128, 128)
        din_g, dout_g = (D // GROUPS, H // GROUPS)
        fan_in = din_g
        bound = 1.0 / np.sqrt(fan_in)
        x_t = jax.random.normal(k_x, (B, S, D), dtype=jnp.float32)
        Wf = jax.random.uniform(k_f, (GROUPS, dout_g, din_g), jnp.float32, -bound, bound)
        Wi = jax.random.uniform(k_i, (GROUPS, dout_g, din_g), jnp.float32, -bound, bound)
        Wh = jax.random.uniform(k_h, (GROUPS, dout_g, din_g), jnp.float32, -bound, bound)
        return {'x_t': x_t, 'Wf': Wf, 'Wi': Wi, 'Wh': Wh}
    _L0_attn_in = _L0_attn_setup()

    def _L0_ffn_setup():
        import jax, jax.numpy as jnp
        import numpy as np
        TOP_K = 2
        key = jax.random.key(seed)
        ks = jax.random.split(key, 5)
        B, T, D, F, E = (4, 256, 128, 512, 8)
        s = 0.02
        return {'x': jax.random.normal(ks[0], (B, T, D), jnp.float32), 'gate_w': jax.random.normal(ks[1], (D, E), jnp.float32) * s, 'w1': jax.random.normal(ks[2], (E, D, F), jnp.float32) * s, 'w3': jax.random.normal(ks[3], (E, D, F), jnp.float32) * s, 'w2': jax.random.normal(ks[4], (E, F, D), jnp.float32) * s}
    _L0_ffn_in = _L0_ffn_setup()
    _d = {'L0_attn_x_t': _L0_attn_in['x_t'], 'L0_attn_Wf': _L0_attn_in['Wf'], 'L0_attn_Wi': _L0_attn_in['Wi'], 'L0_attn_Wh': _L0_attn_in['Wh'], 'L0_ffn_gate_w': _L0_ffn_in['gate_w'], 'L0_ffn_w1': _L0_ffn_in['w1'], 'L0_ffn_w3': _L0_ffn_in['w3'], 'L0_ffn_w2': _L0_ffn_in['w2']}
    _x0 = _d['L0_attn_x_t']
    _d['L0_attn_x_t'] = jax.random.normal(jax.random.fold_in(jax.random.key(seed), 1), (8, 256, 128), dtype=_x0.dtype)
    del _x0
    return _d

def reference(L0_attn_x_t, L0_attn_Wf, L0_attn_Wi, L0_attn_Wh, L0_ffn_gate_w, L0_ffn_w1, L0_ffn_w3, L0_ffn_w2):

    def _L0_attn_ref(x_t, Wf, Wi, Wh):
        import jax, jax.numpy as jnp
        import numpy as np
        EPS = 1e-08
        GROUPS = 128

        def log_g(x):
            return jnp.where(x >= 0, jnp.log(jax.nn.relu(x) + 0.5 + EPS), -jax.nn.softplus(-x) + EPS)

        def grouped_linear(x, W):
            B, S, D = x.shape
            G = W.shape[0]
            xg = x.reshape(B, S, G, D // G)
            y = jnp.einsum('bsgi,goi->bsgo', xg, W)
            return y.reshape(B, S, -1)

        def parallel_scan_log(log_coeffs, log_values):
            a_star = jnp.cumsum(log_coeffs + EPS, axis=1)
            log_h0_plus_b_star = jax.lax.cumlogsumexp(log_values - a_star, axis=1)
            return jnp.exp(a_star + log_h0_plus_b_star)
        f_gate = grouped_linear(x_t, Wf)
        i_gate = grouped_linear(x_t, Wi)
        hidden = grouped_linear(x_t, Wh)
        diff = jax.nn.softplus(-f_gate) - jax.nn.softplus(-i_gate)
        log_f = -jax.nn.softplus(diff)
        log_i = -jax.nn.softplus(-diff)
        log_values = log_i + log_g(hidden)
        h_t = parallel_scan_log(log_f, log_values)
        return h_t

    def _L0_ffn_ref(x, gate_w, w1, w3, w2):
        import jax, jax.numpy as jnp
        import numpy as np
        TOP_K = 2
        logits = jnp.einsum('btd,de->bte', x, gate_w)
        probs = jax.nn.softmax(logits, axis=-1)
        expert_weights, expert_indices = jax.lax.top_k(probs, TOP_K)
        expert_weights = expert_weights / expert_weights.sum(-1, keepdims=True)
        E = w1.shape[0]
        out = jnp.zeros_like(x)
        for i in range(E):
            wi = jnp.where(expert_indices == i, expert_weights, 0.0).sum(-1)
            h = jax.nn.silu(jnp.einsum('btd,df->btf', x, w1[i])) * jnp.einsum('btd,df->btf', x, w3[i])
            out = out + jnp.einsum('btf,fd->btd', h, w2[i]) * wi[..., None]
        return out
    x = L0_attn_x_t
    xn = _layernorm(x, axis=-1)
    x = x + _L0_attn_ref(xn, L0_attn_Wf, L0_attn_Wi, L0_attn_Wh) + _L0_ffn_ref(xn, L0_ffn_gate_w, L0_ffn_w1, L0_ffn_w3, L0_ffn_w2)
    return x

_drawn_inputs = setup_inputs


def setup_inputs(seed=0):
    import zlib

    import numpy as np

    out = dict(_drawn_inputs(seed))
    spreads = {}
    factors = {'L0_ffn_gate_w': 8.0,
     'L0_ffn_w1': 8.0,
     'L0_ffn_w3': 8.0,
     'L0_ffn_w2': 8.0,
     'L0_attn_Wf': 6.197,
     'L0_attn_Wi': 5.353}
    for name, (base, spread) in spreads.items():
        noise = np.random.default_rng([zlib.crc32(name.encode()), seed]).standard_normal(out[name].shape)
        drawn = base * np.exp(spread * noise) if base else spread * noise
        out[name] = jnp.asarray(drawn.astype(out[name].dtype))
    for name, factor in factors.items():
        out[name] = (out[name] * factor).astype(out[name].dtype)
    return out
```

```python
from contextlib import ExitStack

import concourse.bass as bass
from concourse import mybir

ALU = mybir.AluOpType
ACT = mybir.ActivationFunctionType
AX = mybir.AxisListType
F32 = mybir.dt.float32
F16 = mybir.dt.float16
BF16 = mybir.dt.bfloat16
I32 = mybir.dt.int32

P = 128
TOP_K = 2
LN_EPS = 1e-5
LOOP = 4
LAG = 6


def bcast(ap, pattern, offset=0):
    return bass.AP(ap.tensor, ap.offset + offset, [list(ap.ap[0])] + pattern)


def mixed_layer(nc, x, Wf, Wi, Wh, gate_w, w1, w3, w2, out):
    B, S, D = x.shape
    E, _, F = w1.shape
    T = B * S
    NT = T // P
    FC = F // P
    NSET = TOP_K * NT
    NB = T * TOP_K // P + E - 1
    assert D == P and T <= 2 ** 11 and LAG < 2 * LOOP < NB
    HALF = NT // 2

    x_rows = x.rearrange("b (h p) d -> p (b h) d", p=P)
    out_rows = out.rearrange("b (h p) d -> p (b h) d", p=P)
    xn_rows = nc.dram_tensor("xn_rows", [T, D], F32).ap()
    y_rows = nc.dram_tensor("y_rows", [(TOP_K * NT + NB) * P, D], F32).ap()

    with ExitStack() as ctx:
        def sb(name, shape, dt=F32):
            return ctx.enter_context(nc.sbuf_tensor(name, shape, dt))

        def sem(name):
            return ctx.enter_context(nc.semaphore(name))

        w1_sb = sb("w1_sb", [P, E * F])
        w3_sb = sb("w3_sb", [P, E * F])
        w2_sb = sb("w2_sb", [P, E * FC * D])
        gate_sb = sb("gate_sb", [P, E])
        wf_col = sb("wf_col", [P, 1])
        wi_col = sb("wi_col", [P, 1])
        wh_col = sb("wh_col", [P, 1])
        ident = sb("ident", [P, P])
        before = sb("before", [P, P], BF16)
        ones = sb("ones", [P, P], BF16)
        lower_expert = sb("lower_expert", [P, E, E])
        choice_no = sb("choice_no", [P, TOP_K])
        block_edge = sb("block_edge", [P, NT])
        block_no = sb("block_no", [P, NB])
        slot_no = sb("slot_no", [P, P])
        token_no1 = sb("token_no1", [P, NT])
        dump_row = sb("dump_row", [P, NB])
        keep_going = sb("keep_going", [P, E, NT])
        xs = sb("xs", [P, NT, D])
        xc = sb("xc", [P, NT, D])
        xsq = sb("xsq", [P, NT, D])
        xn = sb("xn", [P, NT, D])
        mean = sb("mean", [P, NT])
        var = sb("var", [P, NT])
        root = sb("root", [P, NT])
        newton = sb("newton", [P, NT])
        rstd = sb("rstd", [P, NT])
        logits = sb("logits", [P, NT, E])
        beats = sb("beats", [P, NT, E, E])
        ties = sb("ties", [P, NT, E, E])
        rank = sb("rank", [P, NT, E])
        chosen = sb("chosen", [P, NT, E], BF16)
        is_choice = sb("is_choice", [P, TOP_K, NT, E])
        top_logit = sb("top_logit", [P, TOP_K, NT])
        picked = sb("picked", [P, TOP_K, NT, E])
        share = sb("share", [P, TOP_K, NT])
        gap = sb("gap", [P, NT])
        gap_exp = sb("gap_exp", [P, NT])
        gap_sum = sb("gap_sum", [P, NT])
        count = sb("count", [P, E])
        over_edge = sb("over_edge", [P, E, NT])
        blocks = sb("blocks", [P, E])
        blocks_end = sb("blocks_end", [P, E])
        first_block = sb("first_block", [P, E])
        run_add = sb("run_add", [P, E, NT])
        tile_base = sb("tile_base", [P, E, NT])
        slot_of = sb("slot_of", [P, NT, E])
        slot = sb("slot", [P, NSET])
        slot_i = sb("slot_i", [P, NSET], I32)
        slot_block = sb("slot_block", [P, NSET], I32)
        slot_row = sb("slot_row", [P, NSET], I32)
        in_row = sb("in_row", [P, NSET, P], F16)
        in_block = sb("in_block", [P, NSET, NB], F16)
        inv1 = sb("inv1", [P, TOP_K, NB])
        second = sb("second", [P, NB])
        any1 = sb("any1", [P, NB])
        empty = sb("empty", [P, NB])
        source = sb("source", [P, NB])
        dest_a = sb("dest_a", [P, NB])
        dest_b = sb("dest_b", [P, NB])
        index = sb("index", [P, NB, 2], I32)
        passed = sb("passed", [1, NB, E])
        expert_f = sb("expert_f", [1, NB])
        expert_at = sb("expert_at", [1, NB], I32)
        base = sb("base", [P, NT, D])
        xnT = sb("xnT", [P, T])
        f_gate = sb("f_gate", [P, T])
        i_gate = sb("i_gate", [P, T])
        f_ln = sb("f_ln", [P, T])
        i_ln = sb("i_ln", [P, T])
        hid = sb("hid", [P, T])
        xg = sb("xg", [P, LOOP, D])
        xgT = sb("xgT", [P, LOOP, P])
        silu = sb("silu", [P, LOOP, F])
        hb = sb("hb", [P, LOOP, F])
        hT = sb("hT", [P, LOOP, F])
        yb = sb("yb", [P, LOOP, D])
        idx_in = sb("idx_in", [P, LOOP, 1], I32)
        idx_out = sb("idx_out", [P, LOOP, 1], I32)
        y_first = f_gate[:, :].rearrange("p (t d) -> p t d", d=D)
        y_second = hid[:, :].rearrange("p (t d) -> p t d", d=D)

        bank = [ctx.enter_context(nc.psum_tensor(f"bank{n}", [P, 512], F32)) for n in range(8)]
        gate_ps, up_ps, hT_ps = bank[0:2], bank[2:4], bank[4]
        xgT_ps, y_ps = bank[5][:, 0:P], bank[6][:, 0:P]

        x_in = sem("x_in")
        cols_in = sem("cols_in")
        weights_in = sem("weights_in")
        consts_ready = sem("consts_ready")
        ident_zero = sem("ident_zero")
        ln_step = sem("ln_step")
        squared = sem("squared")
        root_ready = sem("root_ready")
        xn_ready = sem("xn_ready")
        xn_stored = sem("xn_stored")
        xnT_ps_ready = sem("xnT_ps_ready")
        xnT_ready = sem("xnT_ready")
        logits_ready = sem("logits_ready")
        rt = sem("rt")
        chosen_ready = sem("chosen_ready")
        counts_ready = sem("counts_ready")
        gap_ready = sem("gap_ready")
        gap_exp_ready = sem("gap_exp_ready")
        onehots_ready = sem("onehots_ready")
        inverse_ready = sem("inverse_ready")
        index_ready = sem("index_ready")
        expert_ready = sem("expert_ready")
        gru_act = sem("gru_act")
        gru_dve = sem("gru_dve")
        h_ready = sem("h_ready")
        h_tok_ready = sem("h_tok_ready")
        h_tok_used = sem("h_tok_used")
        idx_in_ready = sem("idx_in_ready")
        idx_out_ready = sem("idx_out_ready")
        gathered = [sem(f"gathered{j}") for j in range(LOOP)]
        xgT_ps_ready = sem("xgT_ps_ready")
        xgT_ready = sem("xgT_ready")
        gate_done = sem("gate_done")
        up_done = sem("up_done")
        silu_ready = sem("silu_ready")
        hb_ready = sem("hb_ready")
        hT_ps_ready = sem("hT_ps_ready")
        hT_ready = sem("hT_ready")
        y_ps_ready = sem("y_ps_ready")
        yb_ready = sem("yb_ready")
        scattered = [sem(f"scattered{j}") for j in range(LOOP)]
        y_back = sem("y_back")
        fin = sem("fin")
        out_stored = sem("out_stored")

        block = ctx.enter_context(nc.Block())

        def number(g, c):
            return c if g is None else g * LOOP + c

        def need(eng, what, g, c):
            if g is not None:
                eng.wait_ge(what, g * LOOP + (c + 1))
            elif c >= 0:
                eng.wait_ge(what, c + 1)

        def run_blocks(eng, body, lead):
            turns = (NB - 1 - lead) // LOOP
            for b in range(lead):
                body(None, b)
            with eng.Fori(0, turns) as g:
                for c in range(lead, lead + LOOP):
                    body(g, c)
            for b in range(lead + turns * LOOP, NB):
                body(None, b)

        def landed(eng, what, g, c):
            turns = c // LOOP + 1
            if g is not None:
                eng.wait_ge(what[c % LOOP], g * 16 + 16 * turns)
            elif c >= 0:
                eng.wait_ge(what[c % LOOP], 16 * turns)

        @block.sync
        def _(sp):
            for h in range(2):
                sp.dma_start(xs[:, h * HALF:(h + 1) * HALF, :],
                             x_rows[:, h * HALF:(h + 1) * HALF, :]).then_inc(x_in, 16)
            sp.dma_start(gate_sb[:, :], gate_w).then_inc(cols_in, 16)
            for dst, src in ((wf_col, Wf), (wi_col, Wi), (wh_col, Wh)):
                sp.dma_start(dst[:, :], src.rearrange("g o i -> g (o i)")).then_inc(cols_in, 16)
            sp.dma_start(w1_sb[:, :].rearrange("p (e f) -> p e f", e=E),
                         w1.rearrange("e p f -> p e f")).then_inc(weights_in, 16)
            sp.dma_start(w3_sb[:, :].rearrange("p (e f) -> p e f", e=E),
                         w3.rearrange("e p f -> p e f")).then_inc(weights_in, 16)
            sp.dma_start(w2_sb[:, :].rearrange("p (e c d) -> p e c d", e=E, c=FC),
                         w2.rearrange("e (c p) d -> p e c d", p=P)).then_inc(weights_in, 16)
            sp.wait_ge(xn_ready, 1)
            sp.dma_start(xn_rows.rearrange("(t p) d -> p t d", p=P), xn[:, :, :]).then_inc(xn_stored, 16)
            for j in range(LOOP):
                landed(sp, scattered, None, NB - 1 - (NB - 1 - j) % LOOP)
            for k, dst in enumerate((y_first, y_second)):
                sp.dma_start(dst, y_rows[k * T:(k + 1) * T, :].rearrange("(t p) d -> p t d", p=P)
                             ).then_inc(y_back, 16)
            sp.wait_ge(fin, 4)
            sp.dma_start(out_rows, base[:, :, :]).then_inc(out_stored, 16)
            sp.wait_ge(out_stored, 16)

        @block.gpsimd
        def _(pool):
            nc.gpsimd.memset(ident[:, :], 0.0).then_inc(ident_zero, 1)
            nc.gpsimd.memset(before[:, :], 1.0).then_inc(ident_zero, 1)
            nc.gpsimd.memset(lower_expert[:, :, :], 1.0).then_inc(ident_zero, 1)
            nc.gpsimd.memset(keep_going[:, :, :], 1.0).then_inc(ident_zero, 1)
            nc.gpsimd.memset(ones[:, :], 1.0).then_inc(consts_ready, 1)
            pool.wait_ge(ident_zero, 4)
            nc.gpsimd.affine_select(out=ident[:, :], in_=ident[:, :], compare_op=ALU.not_equal, fill=1.0,
                                    base=0, pattern=[[-1, P]], channel_multiplier=1).then_inc(consts_ready, 1)
            nc.gpsimd.affine_select(out=before[:, :], in_=before[:, :], compare_op=ALU.is_gt, fill=0.0,
                                    base=0, pattern=[[1, P]], channel_multiplier=-1).then_inc(consts_ready, 1)
            nc.gpsimd.affine_select(out=lower_expert[:, :, :], in_=lower_expert[:, :, :], compare_op=ALU.is_gt,
                                    fill=0.0, base=0, pattern=[[1, E], [-1, E]],
                                    channel_multiplier=0).then_inc(consts_ready, 1)
            nc.gpsimd.memset(keep_going[:, :, 0:1], 0.0).then_inc(consts_ready, 1)
            for tile, pattern, start, per_partition in (
                    (choice_no[:, :], [[1, TOP_K]], 0, 0), (block_edge[:, :], [[P, NT]], 0, 0),
                    (block_no[:, :], [[1, NB]], 0, 0), (slot_no[:, :], [[1, P]], 0, 0),
                    (token_no1[:, :], [[P, NT]], 1, 1), (dump_row[:, :], [[P, NB]], TOP_K * T + 1, 1)):
                nc.gpsimd.iota(tile, pattern, base=start, channel_multiplier=per_partition,
                               allow_small_or_imprecise_dtypes=True).then_inc(consts_ready, 1)

            def gather(g, c):
                j = c % LOOP
                need(pool, xgT_ps_ready, g, c - LOOP)
                nc.gpsimd.tensor_copy(idx_in[:, j, :], index[:, bass.ds(number(g, c), 1), 0]).then_inc(idx_in_ready, 1)
                need(pool, idx_in_ready, g, c)
                pool.nop(nofuse=True)
                nc.gpsimd.indirect_dma_start(
                    xg[:, j, :], None, xn_rows, bass.IndirectOffsetOnAxis(ap=idx_in[:, j, :], axis=0)
                ).then_inc(gathered[j], 16)

            def scatter(g, c):
                j = c % LOOP
                landed(pool, scattered, g, c - LOOP)
                nc.gpsimd.tensor_copy(idx_out[:, j, :], index[:, bass.ds(number(g, c), 1), 1]).then_inc(idx_out_ready, 1)
                need(pool, idx_out_ready, g, c)
                need(pool, yb_ready, g, c)
                pool.nop(nofuse=True)
                nc.gpsimd.indirect_dma_start(
                    y_rows, bass.IndirectOffsetOnAxis(ap=idx_out[:, j, :], axis=0), yb[:, j, :], None
                ).then_inc(scattered[j], 16)

            pool.wait_ge(index_ready, 2)
            pool.wait_ge(xn_stored, 16)
            def pool_block(g, c):
                gather(g, c)
                if g is not None or c >= LAG:
                    scatter(g, c - LAG)

            run_blocks(pool, pool_block, LAG + LOOP)
            for b in range(NB - LAG, NB):
                scatter(None, b)

        @block.scalar
        def _(act):
            act.wait_ge(ln_step, 2)
            nc.scalar.activation(xsq[:, :, :], xc[:, :, :], ACT.Square).then_inc(squared, 1)
            act.wait_ge(ln_step, 4)
            nc.scalar.activation(root[:, :], var[:, :], ACT.Sqrt).then_inc(root_ready, 1)
            for q in range(NT // 4):
                act.wait_ge(xnT_ps_ready, q + 1)
                nc.scalar.activation(xnT[:, q * 512:(q + 1) * 512], bank[q][:, :], ACT.Copy).then_inc(xnT_ready, 1)
            act.wait_ge(cols_in, 64)
            act.wait_ge(xnT_ready, NT // 4)
            nc.scalar.activation(f_gate[:, :], xnT[:, :], ACT.Copy, scale=wf_col[:, 0:1]).then_inc(gru_act, 1)
            nc.scalar.activation(i_gate[:, :], xnT[:, :], ACT.Copy, scale=wi_col[:, 0:1]).then_inc(gru_act, 1)
            nc.scalar.activation(f_ln[:, :], xnT[:, :], ACT.Abs, scale=wf_col[:, 0:1]).then_inc(gru_act, 1)
            nc.scalar.activation(i_ln[:, :], xnT[:, :], ACT.Abs, scale=wi_col[:, 0:1]).then_inc(gru_act, 1)
            act.wait_ge(gru_act, 3)
            nc.scalar.activation(f_ln[:, :], f_ln[:, :], ACT.Exp, scale=-1.0).then_inc(gru_act, 1)
            act.wait_ge(gru_act, 4)
            nc.scalar.activation(i_ln[:, :], i_ln[:, :], ACT.Exp, scale=-1.0).then_inc(gru_act, 1)
            act.wait_ge(gap_ready, 1)
            nc.scalar.activation(gap_exp[:, :], gap[:, :], ACT.Exp).then_inc(gap_exp_ready, 1)
            act.wait_ge(gru_act, 5)
            nc.scalar.activation(f_ln[:, :], f_ln[:, :], ACT.Ln, bias=1.0).then_inc(gru_act, 1)
            act.wait_ge(gru_act, 6)
            nc.scalar.activation(i_ln[:, :], i_ln[:, :], ACT.Ln, bias=1.0).then_inc(gru_act, 1)
            nc.scalar.activation(hid[:, :], xnT[:, :], ACT.Sigmoid, scale=wh_col[:, 0:1]).then_inc(gru_act, 1)
            act.wait_ge(gru_dve, 3)
            nc.scalar.activation(i_gate[:, :], f_ln[:, :], ACT.Sigmoid).then_inc(gru_act, 1)
            nc.scalar.activation(f_gate[:, :], f_ln[:, :], ACT.Sigmoid, scale=-1.0).then_inc(gru_act, 1)

            def gate(g, c):
                j = c % LOOP
                need(act, gate_done, g, c)
                need(act, hb_ready, g, c - LOOP)
                nc.scalar.activation(silu[:, j, :], gate_ps[j % 2][:, :], ACT.Silu).then_inc(silu_ready, 1)

            def result(g, c):
                need(act, y_ps_ready, g, c)
                landed(act, scattered, g, c - LOOP)
                nc.scalar.activation(yb[:, c % LOOP, :], y_ps, ACT.Copy).then_inc(yb_ready, 1)

            def act_block(g, c):
                gate(g, c)
                if g is not None or c >= 2:
                    result(g, c - 2)

            run_blocks(act, act_block, 2 + LOOP)
            result(None, NB - 2)
            result(None, NB - 1)

        @block.vector
        def _(dve):
            dve.wait_ge(x_in, 32)
            nc.vector.tensor_reduce(mean[:, :], xs[:, :, :], AX.X, ALU.add, negate=True).then_inc(ln_step, 1)
            dve.wait_ge(ln_step, 1)
            nc.vector.scalar_tensor_tensor(out=xc[:, :, :].rearrange("p t d -> p t d"),
                                           in0=bcast(mean[:, :], [[1, NT], [0, D]]), scalar=1.0 / D,
                                           in1=xs[:, :, :], op0=ALU.mult, op1=ALU.add).then_inc(ln_step, 1)
            dve.wait_ge(squared, 1)
            nc.vector.tensor_reduce(var[:, :], xsq[:, :, :], AX.X, ALU.add).then_inc(ln_step, 1)
            dve.wait_ge(ln_step, 3)
            nc.vector.tensor_scalar(var[:, :], var[:, :], 1.0 / D, LN_EPS, ALU.mult, ALU.add).then_inc(ln_step, 1)
            dve.wait_ge(ln_step, 4)
            dve.wait_ge(root_ready, 1)
            nc.vector.reciprocal(rstd[:, :], root[:, :]).then_inc(ln_step, 1)
            dve.wait_ge(ln_step, 5)
            nc.vector.tensor_tensor(newton[:, :], rstd[:, :], rstd[:, :], ALU.mult).then_inc(ln_step, 1)
            dve.wait_ge(ln_step, 6)
            nc.vector.tensor_tensor(newton[:, :], newton[:, :], var[:, :], ALU.mult).then_inc(ln_step, 1)
            dve.wait_ge(ln_step, 7)
            nc.vector.tensor_scalar(newton[:, :], newton[:, :], -0.5, 1.5, ALU.mult, ALU.add).then_inc(ln_step, 1)
            dve.wait_ge(ln_step, 8)
            nc.vector.tensor_tensor(rstd[:, :], rstd[:, :], newton[:, :], ALU.mult).then_inc(ln_step, 1)
            dve.wait_ge(ln_step, 9)
            nc.vector.tensor_tensor(xn[:, :, :], xc[:, :, :], bcast(rstd[:, :], [[1, NT], [0, D]]),
                                    ALU.mult).then_inc(xn_ready, 1)
            dve.wait_ge(logits_ready, 1)
            nc.vector.tensor_copy(logits[:, :, :].rearrange("p t e -> p (t e)"), bank[4][:, 0:NT * E]).then_inc(rt, 1)
            dve.wait_ge(rt, 1)
            theirs = bcast(logits[:, :, :], [[E, NT], [0, E], [1, E]])
            mine = bcast(logits[:, :, :], [[E, NT], [1, E], [0, E]])
            dve.wait_ge(consts_ready, 11)
            nc.vector.tensor_tensor(beats[:, :, :, :], theirs, mine, ALU.is_gt).then_inc(rt, 1)
            nc.vector.tensor_tensor(ties[:, :, :, :], theirs, mine, ALU.is_equal).then_inc(rt, 1)
            dve.wait_ge(rt, 3)
            nc.vector.tensor_tensor(ties[:, :, :, :].rearrange("p t e j -> p t (e j)"),
                                    ties[:, :, :, :].rearrange("p t e j -> p t (e j)"),
                                    bcast(lower_expert[:, :, :], [[0, NT], [1, E * E]]), ALU.mult).then_inc(rt, 1)
            dve.wait_ge(rt, 4)
            nc.vector.tensor_tensor(beats[:, :, :, :], beats[:, :, :, :], ties[:, :, :, :], ALU.add).then_inc(rt, 1)
            dve.wait_ge(rt, 5)
            nc.vector.tensor_reduce(rank[:, :, :], beats[:, :, :, :], AX.X, ALU.add).then_inc(rt, 1)
            dve.wait_ge(rt, 6)
            nc.vector.tensor_scalar(chosen[:, :, :], rank[:, :, :], float(TOP_K), None, ALU.is_lt).then_inc(chosen_ready, 1)
            nc.vector.tensor_tensor(is_choice[:, :, :, :].rearrange("p k t e -> p k (t e)"),
                                    bcast(rank[:, :, :], [[0, TOP_K], [1, NT * E]]),
                                    bcast(choice_no[:, :], [[1, TOP_K], [0, NT * E]]), ALU.is_equal).then_inc(rt, 1)
            dve.wait_ge(rt, 7)
            nc.vector.tensor_tensor(picked[:, :, :, :].rearrange("p k t e -> p k (t e)"),
                                    is_choice[:, :, :, :].rearrange("p k t e -> p k (t e)"),
                                    bcast(logits[:, :, :], [[0, TOP_K], [1, NT * E]]), ALU.mult).then_inc(rt, 1)
            dve.wait_ge(rt, 8)
            nc.vector.tensor_reduce(top_logit[:, :, :], picked[:, :, :, :], AX.X, ALU.add).then_inc(rt, 1)
            dve.wait_ge(rt, 9)
            nc.vector.tensor_tensor(gap[:, :], top_logit[:, 1, :], top_logit[:, 0, :], ALU.subtract).then_inc(gap_ready, 1)
            dve.wait_ge(gap_exp_ready, 1)
            nc.vector.tensor_scalar(gap_sum[:, :], gap_exp[:, :], 1.0, None, ALU.add).then_inc(rt, 1)
            dve.wait_ge(rt, 10)
            nc.vector.reciprocal(share[:, 0, :], gap_sum[:, :]).then_inc(rt, 1)
            dve.wait_ge(rt, 11)
            nc.vector.tensor_tensor(share[:, 1, :], share[:, 0, :], gap_exp[:, :], ALU.mult).then_inc(rt, 1)
            dve.wait_ge(counts_ready, 1)
            earlier_ps = bank[5][:, 0:NT * E]
            total_ps = bank[6][:, 0:NT * E]
            nc.vector.tensor_reduce(count[:, :], total_ps.rearrange("p (t e) -> p e t", e=E), AX.X, ALU.add).then_inc(rt, 1)
            nc.vector.tensor_copy(run_add[:, :, 1:NT], total_ps.rearrange("p (t e) -> p e t", e=E)[:, :, 0:NT - 1]).then_inc(rt, 1)
            dve.wait_ge(rt, 14)
            nc.vector.tensor_tensor(over_edge[:, :, :], bcast(count[:, :], [[1, E], [0, NT]]),
                                    bcast(block_edge[:, :], [[0, E], [1, NT]]), ALU.is_gt).then_inc(rt, 1)
            dve.wait_ge(rt, 15)
            nc.vector.tensor_reduce(blocks[:, :], over_edge[:, :, :], AX.X, ALU.add).then_inc(rt, 1)
            dve.wait_ge(rt, 16)
            nc.vector.tensor_tensor_scan(blocks_end[:, :], ones[:, 0:E], blocks[:, :], 0.0, ALU.mult, ALU.add).then_inc(rt, 1)
            dve.wait_ge(rt, 17)
            nc.vector.tensor_tensor(first_block[:, :], blocks_end[:, :], blocks[:, :], ALU.subtract).then_inc(rt, 1)
            dve.wait_ge(rt, 18)
            nc.vector.tensor_scalar(run_add[:, :, 0], first_block[:, :], float(P), None, ALU.mult).then_inc(rt, 1)
            dve.wait_ge(rt, 19)
            nc.vector.tensor_tensor_scan(tile_base[:, :, :].rearrange("p e t -> p (e t)"),
                                         keep_going[:, :, :].rearrange("p e t -> p (e t)"),
                                         run_add[:, :, :].rearrange("p e t -> p (e t)"), 0.0, ALU.mult,
                                         ALU.add).then_inc(rt, 1)
            dve.wait_ge(rt, 20)
            nc.vector.tensor_tensor(slot_of[:, :, :], earlier_ps.rearrange("p (t e) -> p t e", e=E),
                                    tile_base[:, :, :].rearrange("p e t -> p t e"), ALU.add).then_inc(rt, 1)
            dve.wait_ge(rt, 21)
            nc.vector.tensor_tensor(picked[:, :, :, :].rearrange("p k t e -> p k (t e)"),
                                    is_choice[:, :, :, :].rearrange("p k t e -> p k (t e)"),
                                    bcast(slot_of[:, :, :], [[0, TOP_K], [1, NT * E]]), ALU.mult).then_inc(rt, 1)
            dve.wait_ge(rt, 22)
            nc.vector.tensor_reduce(slot[:, :].rearrange("p (k t) -> p k t", k=TOP_K), picked[:, :, :, :],
                                    AX.X, ALU.add).then_inc(rt, 1)
            dve.wait_ge(rt, 23)
            nc.vector.tensor_copy(slot_i[:, :], slot[:, :]).then_inc(rt, 1)
            dve.wait_ge(rt, 24)
            nc.vector.tensor_scalar(slot_block[:, :], slot_i[:, :], 7, None, ALU.logical_shift_right).then_inc(rt, 1)
            nc.vector.tensor_scalar(slot_row[:, :], slot_i[:, :], P - 1, None, ALU.bitwise_and).then_inc(rt, 1)
            dve.wait_ge(rt, 25)
            nc.vector.tensor_tensor(in_block[:, :, :], bcast(slot_block[:, :], [[1, NSET], [0, NB]]),
                                    bcast(block_no[:, :], [[0, NSET], [1, NB]]), ALU.is_equal).then_inc(rt, 1)
            dve.wait_ge(rt, 27)
            nc.vector.tensor_tensor(in_row[:, :, :], bcast(slot_row[:, :], [[1, NSET], [0, P]]),
                                    bcast(slot_no[:, :], [[0, NSET], [1, P]]), ALU.is_equal).then_inc(onehots_ready, 1)
            nc.vector.tensor_tensor(in_block[:, :, :].rearrange("p (k t) b -> p k t b", k=TOP_K),
                                    in_block[:, :, :].rearrange("p (k t) b -> p k t b", k=TOP_K),
                                    bcast(token_no1[:, :], [[0, TOP_K], [1, NT], [0, NB]]), ALU.mult).then_inc(onehots_ready, 1)
            nc.vector.tensor_tensor(passed[:, :, :], bcast(block_no[0:1, :], [[1, NB], [0, E]]),
                                    bcast(first_block[0:1, :], [[0, NB], [1, E]]), ALU.is_ge).then_inc(rt, 1)
            dve.wait_ge(rt, 28)
            nc.vector.tensor_reduce(expert_f[:, :], passed[:, :, :], AX.X, ALU.add).then_inc(rt, 1)
            dve.wait_ge(rt, 29)
            nc.vector.tensor_scalar(expert_at[:, :], expert_f[:, :], float(F), -float(F), ALU.mult, ALU.add).then_inc(expert_ready, 1)
            dve.wait_ge(inverse_ready, 1)
            nc.vector.tensor_copy(inv1[:, :, :].rearrange("p k b -> p (k b)"), bank[0][:, 0:TOP_K * NB]).then_inc(rt, 1)
            dve.wait_ge(rt, 30)
            nc.vector.tensor_tensor(any1[:, :], inv1[:, 0, :], inv1[:, 1, :], ALU.add).then_inc(rt, 1)
            nc.vector.tensor_scalar(second[:, :], inv1[:, 1, :], 0.0, float(T), ALU.is_gt, ALU.mult).then_inc(rt, 1)
            dve.wait_ge(rt, 32)
            nc.vector.tensor_scalar(index[:, :, 0], any1[:, :], -1.0, 0.0, ALU.add, ALU.max).then_inc(index_ready, 1)
            nc.vector.scalar_tensor_tensor(out=empty[:, :], in0=any1[:, :], scalar=0.0, in1=dump_row[:, :],
                                           op0=ALU.is_equal, op1=ALU.mult).then_inc(rt, 1)
            nc.vector.scalar_tensor_tensor(out=dest_a[:, :], in0=any1[:, :], scalar=-1.0, in1=second[:, :],
                                           op0=ALU.add, op1=ALU.add).then_inc(rt, 1)
            dve.wait_ge(rt, 34)
            nc.vector.tensor_tensor(index[:, :, 1], dest_a[:, :], empty[:, :], ALU.add).then_inc(index_ready, 1)

            dve.wait_ge(gru_act, 7)
            nc.vector.scalar_tensor_tensor(out=f_gate[:, :], in0=f_gate[:, :], scalar=0.0, in1=f_ln[:, :],
                                           op0=ALU.min, op1=ALU.subtract).then_inc(gru_dve, 1)
            dve.wait_ge(gru_act, 8)
            nc.vector.scalar_tensor_tensor(out=i_gate[:, :], in0=i_gate[:, :], scalar=0.0, in1=i_ln[:, :],
                                           op0=ALU.min, op1=ALU.subtract).then_inc(gru_dve, 1)
            dve.wait_ge(gru_dve, 2)
            nc.vector.tensor_tensor(f_ln[:, :], i_gate[:, :], f_gate[:, :], ALU.subtract).then_inc(gru_dve, 1)
            dve.wait_ge(xnT_ready, NT // 4)
            nc.vector.tensor_scalar(i_ln[:, :], xnT[:, :], wh_col[:, 0:1], 0.0, ALU.mult, ALU.max).then_inc(gru_dve, 1)
            dve.wait_ge(gru_act, 9)
            dve.wait_ge(gru_dve, 4)
            nc.vector.scalar_tensor_tensor(out=hid[:, :], in0=hid[:, :], scalar=0.5, in1=i_ln[:, :],
                                           op0=ALU.min, op1=ALU.add).then_inc(gru_dve, 1)
            dve.wait_ge(gru_act, 10)
            dve.wait_ge(gru_dve, 5)
            nc.vector.tensor_tensor(hid[:, :], hid[:, :], i_gate[:, :], ALU.mult).then_inc(gru_dve, 1)
            dve.wait_ge(gru_act, 11)
            dve.wait_ge(gru_dve, 6)
            for r in range(B):
                seq = slice(r * S, (r + 1) * S)
                nc.vector.tensor_tensor_scan(i_ln[:, seq], f_gate[:, seq], hid[:, seq], 0.0, ALU.mult,
                                             ALU.add).then_inc(h_ready, 1)

            for q in range(NT // 4):
                dve.wait_ge(h_tok_ready, q + 1)
                nc.vector.tensor_tensor(base[:, 4 * q:4 * q + 4, :].rearrange("p t d -> p (t d)"), bank[q][:, :],
                                        xs[:, 4 * q:4 * q + 4, :].rearrange("p t d -> p (t d)"),
                                        ALU.add).then_inc(h_tok_used, 1)

            def turned_x(g, c):
                need(dve, xgT_ps_ready, g, c)
                need(dve, up_done, g, c - LOOP)
                nc.vector.tensor_copy(xgT[:, c % LOOP, :], xgT_ps).then_inc(xgT_ready, 1)

            def gated(g, c):
                j = c % LOOP
                need(dve, up_done, g, c)
                need(dve, silu_ready, g, c)
                need(dve, hT_ps_ready, g, c - LOOP)
                nc.vector.tensor_tensor(hb[:, j, :], silu[:, j, :], up_ps[j % 2][:, :], ALU.mult).then_inc(hb_ready, 1)

            def turned_h(g, c):
                need(dve, hT_ps_ready, g, c)
                need(dve, y_ps_ready, g, c - LOOP)
                nc.vector.tensor_copy(hT[:, c % LOOP, :], hT_ps[:, :]).then_inc(hT_ready, 1)

            def dve_block(g, c):
                if g is not None or c < NB - 1:
                    turned_x(g, c + 1)
                gated(g, c)
                if g is not None or c > 0:
                    turned_h(g, c - 1)

            turned_x(None, 0)
            run_blocks(dve, dve_block, 1 + LOOP)
            turned_h(None, NB - 1)

            dve.wait_ge(y_back, 32)
            dve.wait_ge(rt, 34)
            nc.vector.tensor_tensor(y_first, y_first, bcast(share[:, 0, :], [[1, NT], [0, D]]),
                                    ALU.mult).then_inc(fin, 1)
            nc.vector.tensor_tensor(y_second, y_second, bcast(share[:, 1, :], [[1, NT], [0, D]]),
                                    ALU.mult).then_inc(fin, 1)
            dve.wait_ge(fin, 2)
            nc.vector.tensor_tensor(y_first, y_first, y_second, ALU.add).then_inc(fin, 1)
            dve.wait_ge(fin, 3)
            nc.vector.tensor_tensor(base[:, :, :], base[:, :, :], y_first, ALU.add).then_inc(fin, 1)

        @block.tensor
        def _(pe):
            pe.wait_ge(consts_ready, 11)
            pe.wait_ge(xn_ready, 1)
            for t in range(NT):
                last = nc.tensor.transpose(bank[t // 4][:, (t % 4) * P:(t % 4 + 1) * P], xn[:, t, :], ident[:, :])
                if t % 4 == 3:
                    last.then_inc(xnT_ps_ready, 1)
            pe.wait_ge(cols_in, 64)
            for t in range(NT):
                if t % 4 == 0:
                    pe.wait_ge(xnT_ready, t // 4 + 1)
                last = nc.tensor.matmul(bank[4][:, t * E:(t + 1) * E], xnT[:, t * P:(t + 1) * P], gate_sb[:, :],
                                        start=True, stop=True)
            last.then_inc(logits_ready, 1)
            pe.wait_ge(chosen_ready, 1)
            picks = chosen[:, :, :].rearrange("p t e -> p (t e)")
            nc.tensor.matmul(bank[5][:, 0:NT * E], before[:, :], picks, start=True, stop=True)
            nc.tensor.matmul(bank[6][:, 0:NT * E], ones[:, :], picks, start=True, stop=True).then_inc(counts_ready, 1)
            pe.wait_ge(onehots_ready, 2)
            for k in range(TOP_K):
                for t in range(NT):
                    last = nc.tensor.matmul(bank[0][:, k * NB:(k + 1) * NB], in_row[:, k * NT + t, :],
                                            in_block[:, k * NT + t, :], start=(t == 0), stop=(t == NT - 1))
            last.then_inc(inverse_ready, 1)
            pe.wait_ge(h_ready, B)
            pe.wait_ge(index_ready, 2)
            for t in range(NT):
                last = nc.tensor.transpose(bank[t // 4][:, (t % 4) * P:(t % 4 + 1) * P], i_ln[:, t * P:(t + 1) * P],
                                           ident[:, :])
                if t % 4 == 3:
                    last.then_inc(h_tok_ready, 1)

            def weights_of(g, c):
                return pe.value_load(expert_at[0:1, bass.ds(number(g, c), 1)], min_val=0, max_val=(E - 1) * F)

            def turn_x(g, c):
                landed(pe, gathered, g, c)
                need(pe, xgT_ready, g, c - 1)
                nc.tensor.transpose(xgT_ps, xg[:, c % LOOP, :], ident[:, :]).then_inc(xgT_ps_ready, 1)

            def up(g, c):
                j = c % LOOP
                at = weights_of(g, c)
                need(pe, xgT_ready, g, c)
                need(pe, silu_ready, g, c - 2)
                need(pe, hb_ready, g, c - 2)
                nc.tensor.matmul(gate_ps[j % 2][:, :], xgT[:, j, :], w1_sb[:, bass.ds(at, F)], start=True,
                                 stop=True).then_inc(gate_done, 1)
                nc.tensor.matmul(up_ps[j % 2][:, :], xgT[:, j, :], w3_sb[:, bass.ds(at, F)], start=True,
                                 stop=True).then_inc(up_done, 1)

            def turn_h(g, c):
                need(pe, hb_ready, g, c)
                need(pe, hT_ready, g, c - 1)
                for f in range(FC):
                    last = nc.tensor.transpose(hT_ps[:, f * P:(f + 1) * P], hb[:, c % LOOP, f * P:(f + 1) * P],
                                               ident[:, :])
                last.then_inc(hT_ps_ready, 1)

            def down(g, c):
                at = weights_of(g, c)
                need(pe, hT_ready, g, c)
                need(pe, yb_ready, g, c - 1)
                for f in range(FC):
                    last = nc.tensor.matmul(y_ps, hT[:, c % LOOP, f * P:(f + 1) * P],
                                            w2_sb[:, bass.ds(at + f * D, D)], start=(f == 0), stop=(f == FC - 1))
                last.then_inc(y_ps_ready, 1)

            def pe_block(g, c):
                if g is not None or c < NB - 1:
                    turn_x(g, c + 1)
                up(g, c)
                if g is not None or c > 0:
                    turn_h(g, c - 1)
                if g is not None or c > 1:
                    down(g, c - 2)

            pe.wait_ge(h_tok_used, NT // 4)
            pe.wait_ge(weights_in, 48)
            pe.wait_ge(expert_ready, 1)
            turn_x(None, 0)
            run_blocks(pe, pe_block, LOOP)
            turn_h(None, NB - 1)
            down(None, NB - 2)
            down(None, NB - 1)


_INS = ['L0_attn_x_t', 'L0_attn_Wf', 'L0_attn_Wi', 'L0_attn_Wh', 'L0_ffn_gate_w', 'L0_ffn_w1', 'L0_ffn_w3', 'L0_ffn_w2']
_OUTS = [((8, 256, 128), 'float32')]


def kernel(**inputs):
    import numpy as _np
    import concourse.bacc as _bacc
    from concourse import mybir as _mybir
    from concourse.bass_utils import run_bass_kernel_spmd as _run

    nc = _bacc.Bacc("TRN2", target_bir_lowering=False, num_devices=1)
    arrays, args = {}, []
    for name in _INS:
        a = _np.ascontiguousarray(inputs[name])
        arrays[f"in_{name}_dram"] = a
        args.append(nc.dram_tensor(f"in_{name}_dram", a.shape, _mybir.dt.from_np(a.dtype), kind="ExternalInput").ap())
    for i, (shape, dtype) in enumerate(_OUTS):
        dt = _mybir.dt.from_np(_np.dtype(dtype))
        args.append(nc.dram_tensor(f"out_{i}_dram", shape, dt, kind="ExternalOutput").ap())
    mixed_layer(nc, *args)
    r = _run(nc, [arrays], core_ids=[0])
    got = tuple(r.results[0][f"out_{i}_dram"] for i in range(len(_OUTS)))
    return got[0]
```

```python
from contextlib import ExitStack

import concourse.bass as bass
from concourse import mybir

ALU = mybir.AluOpType
ACT = mybir.ActivationFunctionType
AX = mybir.AxisListType
F32 = mybir.dt.float32
F16 = mybir.dt.float16
BF16 = mybir.dt.bfloat16
I32 = mybir.dt.int32
F32R = mybir.dt.float32r

P = 128
TOP_K = 2
LN_EPS = 1e-5
EPS = 1e-8
LOOP = 4
GATE_CAP = 40.0
MASKED = -3.0e38
WARM_START = 110
WARM_BLOCKS = 30


def bcast(ap, pattern, offset=0):
    return bass.AP(ap.tensor, ap.offset + offset, [list(ap.ap[0])] + pattern)


def mixed_layer(nc, x, Wf, Wi, Wh, gate_w, w1, w3, w2, out):
    B, S, D = x.shape
    E, _, F = w1.shape
    T = B * S
    NT = T // P
    FC = F // P
    NSET = TOP_K * NT
    NB = T * TOP_K // P + E - 1
    assert D == P and T <= 2 ** 11 and 2 * LOOP < NB and S == 2 * P
    ROW = D + TOP_K

    x_rows = x.rearrange("b (h p) d -> p (b h) d", p=P)
    out_rows = out.rearrange("b (h p) d -> p (b h) d", p=P)
    xn_rows = nc.dram_tensor("xn_rows", [T, ROW], F32).ap()
    y_rows = nc.dram_tensor("y_rows", [(TOP_K * NT + NB) * P, D], F32).ap()

    with ExitStack() as ctx:
        def sb(name, shape, dt=F32):
            return ctx.enter_context(nc.sbuf_tensor(name, shape, dt))

        def sem(name):
            return ctx.enter_context(nc.semaphore(name))

        W1, W3, W2 = 0, 1, 2
        HI, LO = 0, 1
        split = sb("split", [P, 2, 3 * E * F], F32R)
        raw = split[:, LO, :].bitcast(F32)
        gate_sb = sb("gate_sb", [P, E])
        gru_cols = sb("gru_cols", [P, 3])
        minus_cols = sb("minus_cols", [P, 3])
        ident = sb("ident", [P, P])
        before = sb("before", [P, P], BF16)
        ones = sb("ones", [P, P], BF16)
        expert_worth = sb("expert_worth", [P, E])
        block_edge = sb("block_edge", [P, NT])
        block_no = sb("block_no", [P, NB])
        slot_no = sb("slot_no", [P, P], F16)
        token_no1 = sb("token_no1", [P, NT])
        dump_row = sb("dump_row", [P, NB])
        keep_going = sb("keep_going", [P, E, NT])
        xs = sb("xs", [P, NT, D])
        xn = sb("xn", [P, NT, ROW])
        stats = sb("stats", [P, NT, 6])
        moments = sb("moments", [P, NT, 2])
        var = sb("var", [P, NT])
        root = sb("root", [P, NT])
        newton = sb("newton", [P, NT])
        rstd = sb("rstd", [P, NT])
        logits = sb("logits", [P, TOP_K, NT, E])
        hits = sb("hits", [P, NT, E])
        worth = sb("worth", [P, NT, E])
        best_worth = sb("best_worth", [P, NT])
        is_choice = sb("is_choice", [P, TOP_K, NT, E])
        chosen = sb("chosen", [P, NT, E], BF16)
        top_logit = sb("top_logit", [P, TOP_K, NT])
        picked = sb("picked", [P, TOP_K, NT, E])
        gap = sb("gap", [P, NT])
        gap_exp = sb("gap_exp", [P, NT])
        gap_sum = sb("gap_sum", [P, NT])
        count = sb("count", [P, E])
        over_edge = sb("over_edge", [P, E, NT])
        blocks = sb("blocks", [P, E])
        blocks_end = sb("blocks_end", [P, E])
        first_block = sb("first_block", [P, E])
        run_add = sb("run_add", [P, E, NT])
        tile_base = sb("tile_base", [P, E, NT])
        slot_of = sb("slot_of", [P, NT, E])
        slot = sb("slot", [P, NSET])
        slot_i = sb("slot_i", [P, NSET], I32)
        slot_block = sb("slot_block", [P, NSET], I32)
        slot_row_i = sb("slot_row_i", [P, NSET], I32)
        slot_row = sb("slot_row", [P, NSET])
        in_row = sb("in_row", [P, NSET, P], F16)
        in_block = sb("in_block", [P, NSET, NB], F16)
        inv1 = sb("inv1", [P, TOP_K, NB])
        second = sb("second", [P, NB])
        is_first = sb("is_first", [P, NB])
        any1 = sb("any1", [P, NB])
        empty = sb("empty", [P, NB])
        dest_a = sb("dest_a", [P, NB])
        index = sb("index", [P, NB, 2], I32)
        passed = sb("passed", [1, NB, E])
        expert_f = sb("expert_f", [1, NB])
        expert_at = sb("expert_at", [1, NB], I32)
        xnT = sb("xnT", [P, T])
        f_part = sb("f_part", [P, T])
        base = xn[:, :, 0:D]
        i_part = sb("i_part", [P, T])
        hid = sb("hid", [P, T])
        relu_seq, keep_seq, value_seq, h_seq = (sb(f"{what}_seq", [P, S]) for what in ("relu", "keep", "value", "h"))
        xg = sb("xg", [P, LOOP, ROW])
        xg_hi = sb("xg_hi", [P, 2, P], F32R)
        xg_lo = sb("xg_lo", [P, 2, P], F32R)
        silu = sb("silu", [P, 2, F])
        hb = sb("hb", [P, 2, F])
        hT_hi = sb("hT_hi", [P, 2, F], F32R)
        hT_lo = sb("hT_lo", [P, 2, F], F32R)
        slot_share = sb("slot_share", [P, 2])
        yb = sb("yb", [P, LOOP, D])
        y_back_at = [raw[:, k * T:(k + 1) * T].rearrange("p (t d) -> p t d", d=D) for k in range(TOP_K)]

        bank = [ctx.enter_context(nc.psum_tensor(f"bank{n}", [P, 512], F32)) for n in range(8)]
        gate_ps, up_ps, hT_ps = bank[0:2], bank[2:4], bank[4]
        xgT_ps, y_ps, h_ps = bank[5][:, 0:P], bank[6][:, 0:2 * P], bank[7][:, 0:S]
        logits_ps, earlier_ps, total_ps = (bank[n][:, 0:NT * E] for n in (4, 5, 6))
        inverse_ps = bank[7][:, 0:TOP_K * NB]
        idle_ps = bank[6][:, 2 * P:3 * P]

        x_in = [sem(f"x_in{q}") for q in range(4)]
        cols_in = sem("cols_in")
        raw_in = [sem(f"raw_in{n}") for n in range(6)]
        consts_zero = sem("consts_zero")
        consts_ready = sem("consts_ready")
        minus_ready = sem("minus_ready")
        stats_ready = sem("stats_ready")
        moments_ready = sem("moments_ready")
        var_ready = sem("var_ready")
        root_ready = sem("root_ready")
        rstd_step = sem("rstd_step")
        xn_ready = sem("xn_ready")
        xn_rest_ready = sem("xn_rest_ready")
        xn_stored = sem("xn_stored")
        xnT_ps_ready = sem("xnT_ps_ready")
        xnT_ready = sem("xnT_ready")
        logits_ready = sem("logits_ready")
        routing_step = sem("routing_step")
        chosen_ready = sem("chosen_ready")
        counts_ready = sem("counts_ready")
        slot_ready = sem("slot_ready")
        gap_ready = sem("gap_ready")
        gap_exp_ready = sem("gap_exp_ready")
        share_step = sem("share_step")
        slot_share_ready = sem("slot_share_ready")
        in_row_ready = sem("in_row_ready")
        in_block_ready = sem("in_block_ready")
        inverse_ready = sem("inverse_ready")
        index_ready = sem("index_ready")
        expert_ready = sem("expert_ready")
        hi_ready = sem("hi_ready")
        lo_ready = sem("lo_ready")
        capped = sem("capped")
        exp_ready = sem("exp_ready")
        ln_ready = sem("ln_ready")
        hid_ready = sem("hid_ready")
        softplus_ready = sem("softplus_ready")
        diff_ready = sem("diff_ready")
        update_ready = sem("update_ready")
        seq_step = sem("seq_step")
        h_seq_ready = sem("h_seq_ready")
        h_ps_ready = sem("h_ps_ready")
        base_ready = sem("base_ready")
        gathered = [sem(f"gathered{j}") for j in range(LOOP)]
        xgT_ps_ready = sem("xgT_ps_ready")
        xg_hi_ready = sem("xg_hi_ready")
        xg_lo_ready = sem("xg_lo_ready")
        gate_done = sem("gate_done")
        up_done = sem("up_done")
        silu_ready = sem("silu_ready")
        hb_ready = sem("hb_ready")
        hT_ps_ready = sem("hT_ps_ready")
        hT_hi_ready = sem("hT_hi_ready")
        hT_lo_ready = sem("hT_lo_ready")
        y_ps_ready = sem("y_ps_ready")
        yb_ready = sem("yb_ready")
        scattered = [sem(f"scattered{j}") for j in range(LOOP)]
        y_back = [sem(f"y_back{q}") for q in range(4)]
        first_added = sem("first_added")
        out_ready = sem("out_ready")
        out_stored = sem("out_stored")

        block = ctx.enter_context(nc.Block())

        QT = NT // 4
        HT = NT // 2
        OWN = HT - 3
        RAW = 4 * F
        NCONST = 10

        def number(g, c):
            return c if g is None else g * LOOP + c

        def need(eng, what, g, c):
            if g is not None:
                eng.wait_ge(what, g * LOOP + (c + 1))
            elif c >= 0:
                eng.wait_ge(what, c + 1)

        def landed(eng, what, g, c):
            turns = c // LOOP + 1
            if g is not None:
                eng.wait_ge(what[c % LOOP], g * 16 + 16 * turns)
            elif c >= 0:
                eng.wait_ge(what[c % LOOP], 16 * turns)

        def run_blocks(eng, body, lead):
            for b in range(lead):
                body(None, b)
            with eng.Fori(0, B) as g:
                for c in range(lead, lead + LOOP):
                    body(g, c)
            for b in range(lead + B * LOOP, NB):
                body(None, b)

        @block.sync
        def _(sp):
            for q in range(4):
                sp.dma_start(xs[:, q * QT:(q + 1) * QT, :], x_rows[:, q * QT:(q + 1) * QT, :]).then_inc(x_in[q], 16)
            sp.dma_start(gate_sb[:, :], gate_w).then_inc(cols_in, 16)
            for n, src in enumerate((Wf, Wi, Wh)):
                sp.dma_start(gru_cols[:, n:n + 1], src.rearrange("g o i -> g (o i)")).then_inc(cols_in, 16)
            for n in range(6):
                experts = slice(n % 2 * 4, n % 2 * 4 + 4)
                dst = raw[:, n * RAW:(n + 1) * RAW]
                if n // 2 == W2:
                    sp.dma_start(dst.rearrange("p (e c d) -> p e c d", e=4, c=FC),
                                 w2[experts].rearrange("e (c p) d -> p e c d", p=P)).then_inc(raw_in[n], 16)
                else:
                    sp.dma_start(dst.rearrange("p (e f) -> p e f", e=4),
                                 (w1, w3)[n // 2][experts].rearrange("e p f -> p e f")).then_inc(raw_in[n], 16)
            sp.wait_ge(xn_ready, 2)
            sp.wait_ge(xn_rest_ready, 2)
            sp.wait_ge(share_step, 3)
            sp.dma_start(xn_rows.rearrange("(t p) d -> p t d", p=P), xn[:, :, :]).then_inc(xn_stored, 16)
            for b in range(NB - LOOP, NB):
                landed(sp, scattered, None, b)
            for q in range(4):
                for k in range(TOP_K):
                    rows = slice(k * T + q * QT * P, k * T + (q + 1) * QT * P)
                    sp.dma_start(y_back_at[k][:, q * QT:(q + 1) * QT, :],
                                 y_rows[rows, :].rearrange("(t p) d -> p t d", p=P)).then_inc(y_back[q], 16)
            for q in range(4):
                sp.wait_ge(out_ready, q + 1)
                sp.dma_start(out_rows[:, q * QT:(q + 1) * QT, :], base[:, q * QT:(q + 1) * QT, :]
                             ).then_inc(out_stored, 16)
            sp.wait_ge(out_stored, 64)

        @block.gpsimd
        def _(pool):
            nc.gpsimd.memset(ident[:, :], 0.0).then_inc(consts_zero, 1)
            nc.gpsimd.memset(before[:, :], 1.0).then_inc(consts_zero, 1)
            nc.gpsimd.memset(keep_going[:, :, :], 1.0).then_inc(consts_zero, 1)
            nc.gpsimd.memset(ones[:, :], 1.0).then_inc(consts_ready, 1)
            pool.wait_ge(consts_zero, 3)
            nc.gpsimd.affine_select(out=ident[:, :], in_=ident[:, :], compare_op=ALU.not_equal, fill=1.0,
                                    base=0, pattern=[[-1, P]], channel_multiplier=1).then_inc(consts_ready, 1)
            nc.gpsimd.affine_select(out=before[:, :], in_=before[:, :], compare_op=ALU.is_gt, fill=0.0,
                                    base=0, pattern=[[1, P]], channel_multiplier=-1).then_inc(consts_ready, 1)
            nc.gpsimd.memset(keep_going[:, :, 0:1], 0.0).then_inc(consts_ready, 1)
            for tile, pattern, start, per_partition in (
                    (expert_worth[:, :], [[-1, E]], E, 0), (block_edge[:, :], [[P, NT]], 0, 0),
                    (block_no[:, :], [[1, NB]], 0, 0), (slot_no[:, :], [[1, P]], 0, 0),
                    (token_no1[:, :], [[P, NT]], 1, 1), (dump_row[:, :], [[P, NB]], TOP_K * T + 1, 1)):
                nc.gpsimd.iota(tile, pattern, base=start, channel_multiplier=per_partition,
                               allow_small_or_imprecise_dtypes=True).then_inc(consts_ready, 1)
            pool.wait_ge(cols_in, 64)
            nc.gpsimd.tensor_scalar(minus_cols[:, :], gru_cols[:, :], -1.0, None, ALU.mult).then_inc(minus_ready, 1)
            for h in range(2):
                pool.wait_ge(rstd_step, 4 * h + 4)
                for t in range(h * HT + OWN, (h + 1) * HT):
                    last = nc.gpsimd.tensor_scalar(xn[:, t, 0:D], xs[:, t, :], moments[:, t, 0:1], rstd[:, t:t + 1],
                                                   ALU.subtract, ALU.mult)
                last.then_inc(xn_rest_ready, 1)

            def low_part(n):
                pool.wait_ge(hi_ready, n + 1)
                at = slice(n * RAW, (n + 1) * RAW)
                nc.gpsimd.tensor_tensor(split[:, LO, at], raw[:, n * RAW:(n + 1) * RAW],
                                        split[:, HI, at].bitcast(F32), ALU.subtract).then_inc(lo_ready, 1)

            for n in range(6):
                low_part(n)

            def gather(b):
                j = b % LOOP
                need(pool, xgT_ps_ready, None, b - LOOP)
                need(pool, slot_share_ready, None, b - LOOP)
                nc.gpsimd.indirect_dma_start(
                    xg[:, j, :], None, xn_rows, bass.IndirectOffsetOnAxis(ap=index[:, b, 0:1], axis=0)
                ).then_inc(gathered[j], 16)

            def scatter(b):
                need(pool, yb_ready, None, b)
                nc.gpsimd.indirect_dma_start(
                    y_rows, bass.IndirectOffsetOnAxis(ap=index[:, b, 1:2], axis=0), yb[:, b % LOOP, :], None
                ).then_inc(scattered[b % LOOP], 16)

            pool.wait_ge(index_ready, 1)
            pool.wait_ge(xn_stored, 16)
            for b in range(LOOP):
                gather(b)
            pool.wait_ge(index_ready, 2)
            for b in range(NB):
                if b + LOOP < NB:
                    gather(b + LOOP)
                if b >= 2:
                    scatter(b - 2)
            scatter(NB - 2)
            scatter(NB - 1)

        @block.scalar
        def _(act):
            nc.scalar.preload_act_table(ACT.Sqrt)

            def high_part(n):
                act.wait_ge(raw_in[n], 16)
                nc.scalar.activation(split[:, HI, n * RAW:(n + 1) * RAW], raw[:, n * RAW:(n + 1) * RAW],
                                     ACT.Copy).then_inc(hi_ready, 1)

            def turned(q):
                act.wait_ge(xnT_ps_ready, q + 1)
                nc.scalar.activation(xnT[:, q * QT * P:(q + 1) * QT * P], bank[q][:, :], ACT.Copy
                                     ).then_inc(xnT_ready, 1)

            def std_of(h):
                act.wait_ge(var_ready, h + 1)
                nc.scalar.activation(root[:, h * HT:(h + 1) * HT], var[:, h * HT:(h + 1) * HT], ACT.Sqrt
                                     ).then_inc(root_ready, 1)

            std_of(0)
            std_of(1)
            nc.scalar.preload_act_table_set("natural_log_exp_and_others")
            turned(0)
            turned(1)
            high_part(0)
            turned(2)
            turned(3)
            for n in range(1, 4):
                high_part(n)
            act.wait_ge(gap_ready, 1)
            nc.scalar.activation(gap_exp[:, :], gap[:, :], ACT.Exp).then_inc(gap_exp_ready, 1)
            high_part(4)
            high_part(5)
            act.wait_ge(capped, 8)
            for part in (f_part[:, :], i_part[:, :]):
                nc.scalar.activation(part, part, ACT.Exp).then_inc(exp_ready, 1)
            for n, part in enumerate((f_part[:, :], i_part[:, :])):
                act.wait_ge(exp_ready, n + 1)
                nc.scalar.activation(part, part, ACT.Ln, bias=1.0).then_inc(ln_ready, 1)
            act.wait_ge(xnT_ready, 4)
            nc.scalar.activation(hid[:, :], xnT[:, :], ACT.Sigmoid, scale=gru_cols[:, 2:3]).then_inc(hid_ready, 1)
            act.wait_ge(diff_ready, 1)
            nc.scalar.activation(i_part[:, :], f_part[:, :], ACT.Sigmoid).then_inc(update_ready, 1)

            def xg_high(g, c):
                need(act, xgT_ps_ready, g, c)
                need(act, up_done, g, c - 2)
                nc.scalar.activation(xg_hi[:, c % 2, :], xgT_ps, ACT.Copy).then_inc(xg_hi_ready, 1)

            def gate(g, c):
                need(act, gate_done, g, c)
                need(act, hb_ready, g, c - 2)
                nc.scalar.activation(silu[:, c % 2, :], gate_ps[c % 2][:, :], ACT.Silu).then_inc(silu_ready, 1)

            def hT_high(g, c):
                need(act, hT_ps_ready, g, c)
                need(act, y_ps_ready, g, c - 2)
                nc.scalar.activation(hT_hi[:, c % 2, :], hT_ps[:, :], ACT.Copy).then_inc(hT_hi_ready, 1)

            def act_block(g, c):
                if g is not None or c < NB - 1:
                    xg_high(g, c + 1)
                gate(g, c)
                if g is not None or c > 0:
                    hT_high(g, c - 1)

            nc.scalar.preload_act_table(ACT.Silu)
            xg_high(None, 0)
            run_blocks(act, act_block, LOOP + 1)
            hT_high(None, NB - 1)

        @block.vector
        def _(dve):
            def stats_of(h):
                for t in range(h * HT, (h + 1) * HT):
                    if t % QT == 0:
                        dve.wait_ge(x_in[t // QT], 16)
                    nc.vector.bn_stats(stats[:, t, :], xs[:, t, :]).then_inc(stats_ready, 1)

            def moments_of(h):
                for t in range(h * HT, (h + 1) * HT):
                    dve.wait_ge(stats_ready, t + 1)
                    nc.vector.bn_aggr(moments[:, t, :], stats[:, t, :]).then_inc(moments_ready, 1)
                dve.wait_ge(moments_ready, (h + 1) * HT)
                nc.vector.tensor_scalar(var[:, h * HT:(h + 1) * HT], moments[:, h * HT:(h + 1) * HT, 1], LN_EPS,
                                        None, ALU.add).then_inc(var_ready, 1)

            def normalised(h):
                at = slice(h * HT, (h + 1) * HT)
                dve.wait_ge(root_ready, h + 1)
                nc.vector.reciprocal(rstd[:, at], root[:, at]).then_inc(rstd_step, 1)
                dve.wait_ge(rstd_step, 4 * h + 1)
                nc.vector.tensor_tensor(newton[:, at], rstd[:, at], rstd[:, at], ALU.mult).then_inc(rstd_step, 1)
                dve.wait_ge(rstd_step, 4 * h + 2)
                nc.vector.scalar_tensor_tensor(out=newton[:, at], in0=var[:, at], scalar=-0.5, in1=newton[:, at],
                                               op0=ALU.mult, op1=ALU.mult).then_inc(rstd_step, 1)
                dve.wait_ge(rstd_step, 4 * h + 3)
                nc.vector.scalar_tensor_tensor(out=rstd[:, at], in0=newton[:, at], scalar=1.5, in1=rstd[:, at],
                                               op0=ALU.add, op1=ALU.mult).then_inc(rstd_step, 1)
                dve.wait_ge(rstd_step, 4 * h + 4)
                for t in range(h * HT, h * HT + OWN):
                    last = nc.vector.tensor_scalar(xn[:, t, 0:D], xs[:, t, :], moments[:, t, 0:1], rstd[:, t:t + 1],
                                                   ALU.subtract, ALU.mult)
                last.then_inc(xn_ready, 1)

            stats_of(0)
            moments_of(0)
            stats_of(1)
            normalised(0)
            moments_of(1)
            normalised(1)

            def capped_gates(q):
                dve.wait_ge(xnT_ready, q + 1)
                at = slice(q * QT * P, (q + 1) * QT * P)
                for n, part in enumerate((f_part, i_part)):
                    nc.vector.tensor_scalar(part[:, at], xnT[:, at], minus_cols[:, n:n + 1], GATE_CAP, ALU.mult,
                                            ALU.min).then_inc(capped, 1)

            dve.wait_ge(minus_ready, 1)
            for q in range(3):
                capped_gates(q)

            def flat(tile):
                return tile.rearrange("p t e -> p (t e)")

            dve.wait_ge(consts_ready, NCONST)
            dve.wait_ge(logits_ready, 4)
            nc.vector.tensor_copy(flat(logits[:, 0, :, :]), logits_ps).then_inc(routing_step, 1)
            dve.wait_ge(routing_step, 1)
            for k in range(TOP_K):
                nc.vector.tensor_reduce(top_logit[:, k, :], logits[:, k, :, :], AX.X, ALU.max
                                        ).then_inc(routing_step, 1)
                dve.wait_ge(routing_step, 6 * k + 2)
                nc.vector.tensor_tensor(hits[:, :, :], logits[:, k, :, :], bcast(top_logit[:, k, :], [[1, NT], [0, E]]),
                                        ALU.is_equal).then_inc(routing_step, 1)
                dve.wait_ge(routing_step, 6 * k + 3)
                nc.vector.tensor_tensor(worth[:, :, :], hits[:, :, :], bcast(expert_worth[:, :], [[0, NT], [1, E]]),
                                        ALU.mult).then_inc(routing_step, 1)
                dve.wait_ge(routing_step, 6 * k + 4)
                nc.vector.tensor_reduce(best_worth[:, :], worth[:, :, :], AX.X, ALU.max).then_inc(routing_step, 1)
                dve.wait_ge(routing_step, 6 * k + 5)
                nc.vector.tensor_tensor(is_choice[:, k, :, :], worth[:, :, :],
                                        bcast(best_worth[:, :], [[1, NT], [0, E]]), ALU.is_equal
                                        ).then_inc(routing_step, 1)
                dve.wait_ge(routing_step, 6 * k + 6)
                if k == 0:
                    nc.vector.scalar_tensor_tensor(out=flat(logits[:, 1, :, :]), in0=flat(is_choice[:, 0, :, :]),
                                                   scalar=MASKED, in1=flat(logits[:, 0, :, :]), op0=ALU.mult,
                                                   op1=ALU.add).then_inc(routing_step, 1)
                    dve.wait_ge(routing_step, 7)
            nc.vector.tensor_tensor(chosen[:, :, :], is_choice[:, 0, :, :], is_choice[:, 1, :, :], ALU.add
                                    ).then_inc(chosen_ready, 1)
            nc.vector.tensor_tensor(gap[:, :], top_logit[:, 1, :], top_logit[:, 0, :], ALU.subtract).then_inc(gap_ready, 1)
            capped_gates(3)
            dve.wait_ge(counts_ready, 1)
            nc.vector.tensor_reduce(count[:, :], total_ps.rearrange("p (t e) -> p e t", e=E), AX.X, ALU.add).then_inc(routing_step, 1)
            nc.vector.tensor_copy(run_add[:, :, 1:NT], total_ps.rearrange("p (t e) -> p e t", e=E)[:, :, 0:NT - 1]).then_inc(routing_step, 1)
            dve.wait_ge(routing_step, 13)
            nc.vector.tensor_tensor(over_edge[:, :, :], bcast(count[:, :], [[1, E], [0, NT]]),
                                    bcast(block_edge[:, :], [[0, E], [1, NT]]), ALU.is_gt).then_inc(routing_step, 1)
            dve.wait_ge(routing_step, 15)
            nc.vector.tensor_reduce(blocks[:, :], over_edge[:, :, :], AX.X, ALU.add).then_inc(routing_step, 1)
            dve.wait_ge(routing_step, 16)
            nc.vector.tensor_tensor_scan(blocks_end[:, :], ones[:, 0:E], blocks[:, :], 0.0, ALU.mult, ALU.add).then_inc(routing_step, 1)
            dve.wait_ge(routing_step, 17)
            nc.vector.tensor_tensor(first_block[:, :], blocks_end[:, :], blocks[:, :], ALU.subtract).then_inc(routing_step, 1)
            dve.wait_ge(routing_step, 18)
            nc.vector.tensor_scalar(run_add[:, :, 0], first_block[:, :], float(P), None, ALU.mult).then_inc(routing_step, 1)
            dve.wait_ge(routing_step, 19)
            nc.vector.tensor_tensor_scan(tile_base[:, :, :].rearrange("p e t -> p (e t)"),
                                         keep_going[:, :, :].rearrange("p e t -> p (e t)"),
                                         run_add[:, :, :].rearrange("p e t -> p (e t)"), 0.0, ALU.mult,
                                         ALU.add).then_inc(routing_step, 1)
            dve.wait_ge(routing_step, 20)
            nc.vector.tensor_tensor(slot_of[:, :, :], earlier_ps.rearrange("p (t e) -> p t e", e=E),
                                    tile_base[:, :, :].rearrange("p e t -> p t e"), ALU.add).then_inc(routing_step, 1)
            dve.wait_ge(routing_step, 21)
            nc.vector.tensor_tensor(picked[:, :, :, :].rearrange("p k t e -> p k (t e)"),
                                    is_choice[:, :, :, :].rearrange("p k t e -> p k (t e)"),
                                    bcast(slot_of[:, :, :], [[0, TOP_K], [1, NT * E]]), ALU.mult).then_inc(routing_step, 1)
            dve.wait_ge(routing_step, 22)
            nc.vector.tensor_reduce(slot[:, :].rearrange("p (k t) -> p k t", k=TOP_K), picked[:, :, :, :],
                                    AX.X, ALU.add).then_inc(routing_step, 1)
            dve.wait_ge(routing_step, 23)
            nc.vector.tensor_copy(slot_i[:, :], slot[:, :]).then_inc(routing_step, 1)
            dve.wait_ge(routing_step, 24)
            nc.vector.tensor_scalar(slot_row_i[:, :], slot_i[:, :], P - 1, None, ALU.bitwise_and).then_inc(slot_ready, 1)
            nc.vector.tensor_scalar(slot_block[:, :], slot_i[:, :], 7, None, ALU.logical_shift_right).then_inc(slot_ready, 1)
            dve.wait_ge(slot_ready, 2)
            nc.vector.tensor_copy(slot_row[:, :], slot_row_i[:, :]).then_inc(slot_ready, 1)
            dve.wait_ge(gap_exp_ready, 1)
            nc.vector.tensor_scalar(gap_sum[:, :], gap_exp[:, :], 1.0, None, ALU.add).then_inc(share_step, 1)
            dve.wait_ge(share_step, 1)
            nc.vector.reciprocal(xn[:, :, D], gap_sum[:, :]).then_inc(share_step, 1)
            dve.wait_ge(share_step, 2)
            nc.vector.tensor_tensor(xn[:, :, D + 1], xn[:, :, D], gap_exp[:, :], ALU.mult).then_inc(share_step, 1)
            nc.vector.tensor_tensor(in_block[:, :, :], bcast(slot_block[:, :], [[1, NSET], [0, NB]]),
                                    bcast(block_no[:, :], [[0, NSET], [1, NB]]), ALU.is_equal).then_inc(routing_step, 1)
            dve.wait_ge(routing_step, 25)
            nc.vector.tensor_tensor(in_block[:, :, :].rearrange("p (k t) b -> p k t b", k=TOP_K),
                                    in_block[:, :, :].rearrange("p (k t) b -> p k t b", k=TOP_K),
                                    bcast(token_no1[:, :], [[0, TOP_K], [1, NT], [0, NB]]), ALU.mult).then_inc(in_block_ready, 1)
            dve.wait_ge(slot_ready, 3)
            for n in range(NSET):
                nc.vector.tensor_scalar(in_row[:, n, :], slot_no[:, :], slot_row[:, n:n + 1], None, ALU.is_equal
                                        ).then_inc(in_row_ready, 1)
            nc.vector.tensor_tensor(passed[:, :, :], bcast(block_no[0:1, :], [[1, NB], [0, E]]),
                                    bcast(first_block[0:1, :], [[0, NB], [1, E]]), ALU.is_ge).then_inc(routing_step, 1)
            dve.wait_ge(routing_step, 26)
            nc.vector.tensor_reduce(expert_f[:, :], passed[:, :, :], AX.X, ALU.add).then_inc(routing_step, 1)
            dve.wait_ge(routing_step, 27)
            nc.vector.tensor_scalar(expert_at[:, :], expert_f[:, :], float(F), -float(F), ALU.mult, ALU.add).then_inc(expert_ready, 1)
            def softplus(n, part):
                dve.wait_ge(ln_ready, n + 1)
                nc.vector.scalar_tensor_tensor(out=part, in0=xnT[:, :], scalar=minus_cols[:, n:n + 1],
                                               in1=part, op0=ALU.mult, op1=ALU.max).then_inc(softplus_ready, 1)

            softplus(0, f_part[:, :])
            dve.wait_ge(inverse_ready, 1)
            nc.vector.tensor_copy(inv1[:, :, :].rearrange("p k b -> p (k b)"), inverse_ps).then_inc(routing_step, 1)
            dve.wait_ge(routing_step, 28)
            nc.vector.tensor_tensor(any1[:, :], inv1[:, 0, :], inv1[:, 1, :], ALU.add).then_inc(routing_step, 1)
            nc.vector.tensor_scalar(is_first[:, :], inv1[:, 1, :], 0.0, None, ALU.is_equal)
            nc.vector.tensor_scalar(second[:, :], inv1[:, 1, :], 0.0, float(T), ALU.is_gt, ALU.mult).then_inc(routing_step, 1)
            dve.wait_ge(routing_step, 30)
            nc.vector.tensor_scalar(index[:, :, 0], any1[:, :], -1.0, 0.0, ALU.add, ALU.max).then_inc(index_ready, 1)
            nc.vector.scalar_tensor_tensor(out=empty[:, :], in0=any1[:, :], scalar=0.0, in1=dump_row[:, :],
                                           op0=ALU.is_equal, op1=ALU.mult).then_inc(routing_step, 1)
            nc.vector.scalar_tensor_tensor(out=dest_a[:, :], in0=any1[:, :], scalar=-1.0, in1=second[:, :],
                                           op0=ALU.add, op1=ALU.add).then_inc(routing_step, 1)
            dve.wait_ge(routing_step, 32)
            nc.vector.tensor_tensor(index[:, :, 1], dest_a[:, :], empty[:, :], ALU.add).then_inc(index_ready, 1)

            softplus(1, i_part[:, :])
            dve.wait_ge(softplus_ready, 2)
            nc.vector.tensor_tensor(f_part[:, :], f_part[:, :], i_part[:, :], ALU.subtract).then_inc(diff_ready, 1)

            def share_of(g, c):
                landed(dve, gathered, g, c)
                need(dve, hb_ready, g, c - 2)
                nc.vector.scalar_tensor_tensor(out=slot_share[:, c % 2:c % 2 + 1], in0=xg[:, c % LOOP, D:D + 1],
                                               scalar=is_first[:, bass.ds(number(g, c), 1)],
                                               in1=xg[:, c % LOOP, D + 1:D + 2], op0=ALU.mult, op1=ALU.max
                                               ).then_inc(slot_share_ready, 1)

            def xg_low(g, c):
                need(dve, xg_hi_ready, g, c)
                need(dve, up_done, g, c - 2)
                nc.vector.tensor_tensor(xg_lo[:, c % 2, :], xgT_ps, xg_hi[:, c % 2, :].bitcast(F32), ALU.subtract
                                        ).then_inc(xg_lo_ready, 1)

            def gated(g, c):
                need(dve, up_done, g, c)
                need(dve, silu_ready, g, c)
                need(dve, hT_ps_ready, g, c - 2)
                need(dve, slot_share_ready, g, c)
                nc.vector.scalar_tensor_tensor(out=hb[:, c % 2, :], in0=silu[:, c % 2, :],
                                               scalar=slot_share[:, c % 2:c % 2 + 1], in1=up_ps[c % 2][:, :],
                                               op0=ALU.mult, op1=ALU.mult).then_inc(hb_ready, 1)

            def hT_low(g, c):
                need(dve, hT_hi_ready, g, c)
                need(dve, y_ps_ready, g, c - 2)
                nc.vector.tensor_tensor(hT_lo[:, c % 2, :], hT_ps[:, :], hT_hi[:, c % 2, :].bitcast(F32), ALU.subtract
                                        ).then_inc(hT_lo_ready, 1)

            def result(g, c):
                need(dve, y_ps_ready, g, c)
                landed(dve, scattered, g, c - LOOP)
                nc.vector.tensor_reduce(yb[:, c % LOOP, :], y_ps.rearrange("p (n d) -> p d n", n=2), AX.X, ALU.add
                                        ).then_inc(yb_ready, 1)

            def gated_update(r):
                seq = bass.ds(r * S, S)
                nc.vector.tensor_scalar(relu_seq[:, :], xnT[:, seq], gru_cols[:, 2:3], 0.0, ALU.mult, ALU.max
                                        ).then_inc(seq_step, 1)
                nc.vector.tensor_scalar(keep_seq[:, :], i_part[:, seq], -1.0 - EPS, 1.0 + EPS, ALU.mult, ALU.add
                                        ).then_inc(seq_step, 1)
                dve.wait_ge(seq_step, r * 4 + 2)
                nc.vector.scalar_tensor_tensor(out=value_seq[:, :], in0=hid[:, seq], scalar=0.5 + EPS, in1=relu_seq[:, :],
                                               op0=ALU.min, op1=ALU.add).then_inc(seq_step, 1)

            def scanned(r):
                seq = bass.ds(r * S, S)
                dve.wait_ge(seq_step, r * 4 + 3)
                nc.vector.tensor_tensor(value_seq[:, :], value_seq[:, :], i_part[:, seq], ALU.mult
                                        ).then_inc(seq_step, 1)
                dve.wait_ge(seq_step, r * 4 + 4)
                nc.vector.tensor_tensor_scan(h_seq[:, :], keep_seq[:, :], value_seq[:, :], 0.0, ALU.mult, ALU.add
                                             ).then_inc(h_seq_ready, 1)

            def added(r):
                dve.wait_ge(h_ps_ready, r + 1)
                tiles = bass.ds(r * (S // P), S // P)
                nc.vector.tensor_tensor(base[:, tiles, :], h_ps.rearrange("p (t d) -> p t d", d=D), xs[:, tiles, :],
                                        ALU.add).then_inc(base_ready, 1)

            def dve_block(g, c):
                if g is not None or c < NB - 1:
                    share_of(g, c + 1)
                    xg_low(g, c + 1)
                if g is not None and c % LOOP == 2:
                    gated_update(g)
                if g is not None and c % LOOP == 1:
                    added(g)
                gated(g, c)
                if g is not None or c > 0:
                    hT_low(g, c - 1)
                if g is not None or c > 1:
                    result(g, c - 2)
                if g is not None and c % LOOP == 2:
                    scanned(g)

            dve.wait_ge(hid_ready, 1)
            dve.wait_ge(update_ready, 1)
            share_of(None, 0)
            xg_low(None, 0)
            run_blocks(dve, dve_block, LOOP + 2)
            hT_low(None, NB - 1)
            result(None, NB - 2)
            result(None, NB - 1)

            dve.wait_ge(base_ready, B)
            for q in range(4):
                tiles = slice(q * QT, (q + 1) * QT)
                dve.wait_ge(y_back[q], 32)
                nc.vector.tensor_tensor(base[:, tiles, :], base[:, tiles, :], y_back_at[0][:, tiles, :], ALU.add
                                        ).then_inc(first_added, 1)
                dve.wait_ge(first_added, q + 1)
                nc.vector.tensor_tensor(base[:, tiles, :], base[:, tiles, :], y_back_at[1][:, tiles, :], ALU.add
                                        ).then_inc(out_ready, 1)

        @block.tensor
        def _(pe):
            pe.wait_ge(consts_ready, NCONST)
            pe.wait_ge(cols_in, 64)

            def stay_warm(count):
                for _ in range(count):
                    nc.tensor.matmul(idle_ps, ones[:, :], before[:, :], start=True, stop=True)

            def logits_of(q):
                pe.wait_ge(xnT_ready, q + 1)
                for t in range(q * QT, (q + 1) * QT):
                    last = nc.tensor.matmul(logits_ps[:, t * E:(t + 1) * E], xnT[:, t * P:(t + 1) * P], gate_sb[:, :],
                                            start=True, stop=True)
                last.then_inc(logits_ready, 1)

            stay_warm(WARM_START)
            for q in range(4):
                pe.wait_ge(xn_ready, q // 2 + 1)
                pe.wait_ge(xn_rest_ready, q // 2 + 1)
                for t in range(q * QT, (q + 1) * QT):
                    last = nc.tensor.transpose(bank[q][:, (t % QT) * P:(t % QT + 1) * P], xn[:, t, 0:D], ident[:, :])
                last.then_inc(xnT_ps_ready, 1)
                if q > 0:
                    logits_of(q - 1)
            logits_of(3)
            pe.wait_ge(chosen_ready, 1)
            picks = chosen[:, :, :].rearrange("p t e -> p (t e)")
            nc.tensor.matmul(earlier_ps, before[:, :], picks, start=True, stop=True)
            nc.tensor.matmul(total_ps, ones[:, :], picks, start=True, stop=True).then_inc(counts_ready, 1)
            pe.wait_ge(in_block_ready, 1)
            for k in range(TOP_K):
                for t in range(NT):
                    pe.wait_ge(in_row_ready, k * NT + t + 1)
                    last = nc.tensor.matmul(inverse_ps[:, k * NB:(k + 1) * NB], in_row[:, k * NT + t, :],
                                            in_block[:, k * NT + t, :], start=(t == 0), stop=(t == NT - 1))
            last.then_inc(inverse_ready, 1)
            stay_warm(WARM_BLOCKS)

            def weights_of(name, first, count):
                regs = [pe.alloc_register(f"{name}_at{n}") for n in range(count)]
                pe.reg_load(regs, expert_at[0:1, bass.ds(first, count)])
                return [pe.snap(reg, donate=True, min_val=0, max_val=(E - 1) * F) for reg in regs]

            def weights(part, at, width):
                return split[:, part, bass.ds(at, width)]

            def product(out_ps, j, at):
                nc.tensor.matmul(out_ps, xg_hi[:, j, :], weights(HI, at, F), start=True, stop=False)
                nc.tensor.matmul(out_ps, xg_hi[:, j, :], weights(LO, at, F), start=False, stop=False)
                return nc.tensor.matmul(out_ps, xg_lo[:, j, :], weights(HI, at, F), start=False, stop=True)

            def turn_x(g, c):
                landed(pe, gathered, g, c)
                need(pe, xg_lo_ready, g, c - 1)
                nc.tensor.transpose(xgT_ps, xg[:, c % LOOP, 0:D], ident[:, :]).then_inc(xgT_ps_ready, 1)

            def up(g, c, at):
                j = c % 2
                need(pe, xg_lo_ready, g, c)
                need(pe, silu_ready, g, c - 2)
                need(pe, hb_ready, g, c - 2)
                product(gate_ps[j][:, :], j, at + W1 * E * F).then_inc(gate_done, 1)
                product(up_ps[j][:, :], j, at + W3 * E * F).then_inc(up_done, 1)

            def turn_h(g, c):
                need(pe, hb_ready, g, c)
                need(pe, hT_lo_ready, g, c - 1)
                for f in range(FC):
                    last = nc.tensor.transpose(hT_ps[:, f * P:(f + 1) * P], hb[:, c % 2, f * P:(f + 1) * P],
                                               ident[:, :])
                last.then_inc(hT_ps_ready, 1)

            def down(g, c, at):
                j = c % 2
                need(pe, hT_lo_ready, g, c)
                need(pe, yb_ready, g, c - 1)
                for f in range(FC):
                    rows = slice(f * P, (f + 1) * P)
                    w_at = at + (W2 * E * F + f * D)
                    nc.tensor.matmul(y_ps.rearrange("p (n d) -> p n d", n=2), hT_hi[:, j, rows],
                                     split[:, :, bass.ds(w_at, D)], start=(f == 0), stop=False)
                    last = nc.tensor.matmul(y_ps[:, P:2 * P], hT_lo[:, j, rows], weights(HI, w_at, D),
                                            start=False, stop=(f == FC - 1))
                last.then_inc(y_ps_ready, 1)

            def turn_seq(r):
                pe.wait_ge(h_seq_ready, r + 1)
                for t in range(S // P):
                    last = nc.tensor.transpose(h_ps[:, t * P:(t + 1) * P], h_seq[:, t * P:(t + 1) * P], ident[:, :])
                last.then_inc(h_ps_ready, 1)

            def pe_block(g, c, weights_at):
                if g is not None or c > 1:
                    turn_h(g, c - 2)
                if g is not None or c > 2:
                    down(g, c - 3, weights_at[-4])
                if g is not None or c < NB - 1:
                    turn_x(g, c + 1)
                up(g, c, weights_at[-1])
                if g is not None and c % LOOP == 3:
                    turn_seq(g)

            pe.wait_ge(expert_ready, 1)
            pe.wait_ge(index_ready, 1)
            pe.wait_ge(lo_ready, 6)
            weights_at = weights_of("first", 0, LOOP)
            turn_x(None, 0)
            for c in range(LOOP):
                pe_block(None, c, weights_at[:c + 1])
            with pe.Fori(0, B) as g:
                weights_at = weights_of("turn", g * LOOP + 1, 2 * LOOP - 1)
                for c in range(LOOP, 2 * LOOP):
                    pe_block(g, c, weights_at[:c])
            after = LOOP * (B + 1)
            weights_at = weights_of("last", after - 3, NB - after + 3)
            for c in range(after, NB):
                pe_block(None, c, weights_at[:c - after + 4])
            turn_h(None, NB - 2)
            down(None, NB - 3, weights_at[-3])
            turn_h(None, NB - 1)
            down(None, NB - 2, weights_at[-2])
            down(None, NB - 1, weights_at[-1])


_INS = ['L0_attn_x_t', 'L0_attn_Wf', 'L0_attn_Wi', 'L0_attn_Wh', 'L0_ffn_gate_w', 'L0_ffn_w1', 'L0_ffn_w3', 'L0_ffn_w2']
_OUTS = [((8, 256, 128), 'float32')]


def kernel(**inputs):
    import numpy as _np
    import concourse.bacc as _bacc
    from concourse import mybir as _mybir
    from concourse.bass_utils import run_bass_kernel_spmd as _run

    nc = _bacc.Bacc("TRN2", target_bir_lowering=False, num_devices=1)
    arrays, args = {}, []
    for name in _INS:
        a = _np.ascontiguousarray(inputs[name])
        arrays[f"in_{name}_dram"] = a
        args.append(nc.dram_tensor(f"in_{name}_dram", a.shape, _mybir.dt.from_np(a.dtype), kind="ExternalInput").ap())
    for i, (shape, dtype) in enumerate(_OUTS):
        dt = _mybir.dt.from_np(_np.dtype(dtype))
        args.append(nc.dram_tensor(f"out_{i}_dram", shape, dt, kind="ExternalOutput").ap())
    mixed_layer(nc, *args)
    r = _run(nc, [arrays], core_ids=[0])
    got = tuple(r.results[0][f"out_{i}_dram"] for i in range(len(_OUTS)))
    return got[0]
```

```python
from contextlib import ExitStack

import concourse.bass as bass
from concourse import mybir

ALU = mybir.AluOpType
ACT = mybir.ActivationFunctionType
AX = mybir.AxisListType
F32 = mybir.dt.float32
F16 = mybir.dt.float16
BF16 = mybir.dt.bfloat16
I32 = mybir.dt.int32
F32R = mybir.dt.float32r

P = 128
TOP_K = 2
LN_EPS = 1e-5
EPS = 1e-8
LOOP = 4
GATE_CAP = 40.0
MASKED = -3.0e38
WARM_START = 85
WARM_TURN = 6
WARM_INVERSE = 115
WARM_BLOCKS = 60


def bcast(ap, pattern, offset=0):
    return bass.AP(ap.tensor, ap.offset + offset, [list(ap.ap[0])] + pattern)


def mixed_layer(nc, x, Wf, Wi, Wh, gate_w, w1, w3, w2, out):
    B, S, D = x.shape
    E, _, F = w1.shape
    T = B * S
    NT = T // P
    FC = F // P
    NSET = TOP_K * NT
    NB = T * TOP_K // P + E - 1
    assert D == P and T <= 2 ** 11 and 2 * LOOP < NB and S == 2 * P
    ROW = D + TOP_K

    x_rows = x.rearrange("b (h p) d -> p (b h) d", p=P)
    out_rows = out.rearrange("b (h p) d -> p (b h) d", p=P)
    xn_rows = nc.dram_tensor("xn_rows", [T, ROW], F32).ap()
    y_rows = nc.dram_tensor("y_rows", [(TOP_K * NT + NB) * P, D], F32).ap()

    with ExitStack() as ctx:
        def sb(name, shape, dt=F32):
            return ctx.enter_context(nc.sbuf_tensor(name, shape, dt))

        def sem(name):
            return ctx.enter_context(nc.semaphore(name))

        W1, W3, W2 = 0, 1, 2
        HI, LO = 0, 1
        split = sb("split", [P, 2, 3 * E * F], F32R)
        raw = split[:, LO, :].bitcast(F32)
        gate_sb = sb("gate_sb", [P, E])
        gru_cols = sb("gru_cols", [P, 3])
        minus_cols = sb("minus_cols", [P, 3])
        ident = sb("ident", [P, P])
        before = sb("before", [P, P], BF16)
        ones = sb("ones", [P, P], BF16)
        expert_worth = sb("expert_worth", [P, E])
        block_edge = sb("block_edge", [P, NT])
        block_no = sb("block_no", [P, NB])
        count_up = sb("count_up", [P, P])
        row_no = sb("row_no", [P, P, NSET], F16)
        block_no_of = sb("block_no_of", [P, NB, NSET], F16)
        token_no1 = sb("token_no1", [P, NSET], F16)
        dump_row = sb("dump_row", [P, NB])
        keep_going = sb("keep_going", [P, E, NT])
        xs = sb("xs", [P, NT, D])
        xn = sb("xn", [P, NT, ROW])
        stats = sb("stats", [P, NT, 6])
        moments = sb("moments", [P, NT, 2])
        var = sb("var", [P, NT])
        root = sb("root", [P, NT])
        newton = sb("newton", [P, NT])
        rstd = sb("rstd", [P, NT])
        logits = sb("logits", [P, TOP_K, NT, E])
        hits = sb("hits", [P, NT, E])
        worth = sb("worth", [P, NT, E])
        best_worth = sb("best_worth", [P, NT])
        is_choice = sb("is_choice", [P, TOP_K, NT, E])
        chosen = sb("chosen", [P, NT, E], BF16)
        top_logit = sb("top_logit", [P, TOP_K, NT])
        picked = sb("picked", [P, TOP_K, NT, E])
        gap = sb("gap", [P, NT])
        gap_exp = sb("gap_exp", [P, NT])
        gap_sum = sb("gap_sum", [P, NT])
        count = sb("count", [P, E])
        over_edge = sb("over_edge", [P, E, NT])
        blocks = sb("blocks", [P, E])
        blocks_end = sb("blocks_end", [P, E])
        first_block = sb("first_block", [P, E])
        run_add = sb("run_add", [P, E, NT])
        tile_base = sb("tile_base", [P, E, NT])
        slot_of = sb("slot_of", [P, NT, E])
        slot = sb("slot", [P, NSET])
        slot_i = sb("slot_i", [P, NSET], I32)
        slot_block_i = sb("slot_block_i", [P, NSET], I32)
        slot_block = sb("slot_block", [P, NSET], F16)
        slot_row_i = sb("slot_row_i", [P, NSET], I32)
        slot_row = sb("slot_row", [P, NSET], F16)
        in_row = sb("in_row", [P, P, NSET], F16)
        in_block = sb("in_block", [P, NB, NSET], F16)
        inv1 = sb("inv1", [P, TOP_K, NB])
        second = sb("second", [P, NB])
        is_first = sb("is_first", [P, NB])
        any1 = sb("any1", [P, NB])
        empty = sb("empty", [P, NB])
        dest_a = sb("dest_a", [P, NB])
        index = sb("index", [P, NB, 2], I32)
        passed = sb("passed", [1, NB, E])
        expert_f = sb("expert_f", [1, NB])
        expert_at = sb("expert_at", [1, NB], I32)
        xnT = sb("xnT", [P, T])
        f_part = sb("f_part", [P, T])
        base = xn[:, :, 0:D]
        i_part = sb("i_part", [P, T])
        hid = sb("hid", [P, T])
        relu_seq, keep_seq, value_seq, h_seq = (sb(f"{what}_seq", [P, S]) for what in ("relu", "keep", "value", "h"))
        xg = sb("xg", [P, LOOP, ROW])
        xg_hi = sb("xg_hi", [P, 2, P], F32R)
        xg_lo = sb("xg_lo", [P, 2, P], F32R)
        silu = sb("silu", [P, 2, F])
        hb = sb("hb", [P, 2, F])
        hT_hi = sb("hT_hi", [P, 2, F], F32R)
        hT_lo = sb("hT_lo", [P, 2, F], F32R)
        slot_share = sb("slot_share", [P, 2])
        yb = sb("yb", [P, LOOP, D])
        y_back_at = [raw[:, k * T:(k + 1) * T].rearrange("p (t d) -> p t d", d=D) for k in range(TOP_K)]

        bank = [ctx.enter_context(nc.psum_tensor(f"bank{n}", [P, 512], F32)) for n in range(8)]
        gate_ps, up_ps, hT_ps = bank[0:2], bank[2:4], bank[4]
        xgT_ps, y_ps, h_ps = bank[5][:, 0:P], bank[6][:, 0:2 * P], bank[7][:, 0:S]
        logits_ps, earlier_ps, total_ps = (bank[n][:, 0:NT * E] for n in (4, 5, 6))
        inverse_ps = bank[7][:, 0:TOP_K * NB]

        x_in = [sem(f"x_in{q}") for q in range(4)]
        cols_in = sem("cols_in")
        raw_in = [sem(f"raw_in{n}") for n in range(6)]
        count_up_ready = sem("count_up_ready")
        numbers_ready = sem("numbers_ready")
        consts_zero = sem("consts_zero")
        consts_ready = sem("consts_ready")
        minus_ready = sem("minus_ready")
        stats_ready = sem("stats_ready")
        moments_ready = sem("moments_ready")
        var_ready = sem("var_ready")
        root_ready = sem("root_ready")
        rstd_step = sem("rstd_step")
        xn_ready = sem("xn_ready")
        xn_stored = sem("xn_stored")
        xnT_ps_ready = sem("xnT_ps_ready")
        xnT_ready = sem("xnT_ready")
        logits_ready = sem("logits_ready")
        routing_step = sem("routing_step")
        chosen_ready = sem("chosen_ready")
        counts_ready = sem("counts_ready")
        slot_ready = sem("slot_ready")
        gap_ready = sem("gap_ready")
        gap_exp_ready = sem("gap_exp_ready")
        share_step = sem("share_step")
        slot_share_ready = sem("slot_share_ready")
        in_row_ready = sem("in_row_ready")
        in_block_ready = sem("in_block_ready")
        inverse_ready = sem("inverse_ready")
        index_ready = sem("index_ready")
        expert_ready = sem("expert_ready")
        hi_ready = sem("hi_ready")
        lo_ready = sem("lo_ready")
        capped = sem("capped")
        exp_ready = sem("exp_ready")
        ln_ready = sem("ln_ready")
        hid_ready = sem("hid_ready")
        softplus_ready = sem("softplus_ready")
        diff_ready = sem("diff_ready")
        update_ready = sem("update_ready")
        seq_step = sem("seq_step")
        h_seq_ready = sem("h_seq_ready")
        h_ps_ready = sem("h_ps_ready")
        base_ready = sem("base_ready")
        gathered = [sem(f"gathered{j}") for j in range(LOOP)]
        xgT_ps_ready = sem("xgT_ps_ready")
        xg_hi_ready = sem("xg_hi_ready")
        xg_lo_ready = sem("xg_lo_ready")
        gate_done = sem("gate_done")
        up_done = sem("up_done")
        silu_ready = sem("silu_ready")
        hb_ready = sem("hb_ready")
        hT_ps_ready = sem("hT_ps_ready")
        hT_hi_ready = sem("hT_hi_ready")
        hT_lo_ready = sem("hT_lo_ready")
        y_ps_ready = sem("y_ps_ready")
        yb_ready = sem("yb_ready")
        scattered = [sem(f"scattered{j}") for j in range(LOOP)]
        y_back = [sem(f"y_back{n}") for n in range(2 + 4)]
        first_added = sem("first_added")
        out_ready = sem("out_ready")
        out_stored = sem("out_stored")

        block = ctx.enter_context(nc.Block())

        QT = NT // 4
        HT = NT // 2
        RAW = 4 * F
        NCONST = 9

        halves = [slice(0, T // 2), slice(T // 2, T)]

        def number(g, c):
            return c if g is None else g * LOOP + c

        def need(eng, what, g, c):
            if g is not None:
                eng.wait_ge(what, g * LOOP + (c + 1))
            elif c >= 0:
                eng.wait_ge(what, c + 1)

        def landed(eng, what, g, c):
            turns = c // LOOP + 1
            if g is not None:
                eng.wait_ge(what[c % LOOP], g * 16 + 16 * turns)
            elif c >= 0:
                eng.wait_ge(what[c % LOOP], 16 * turns)

        def run_blocks(eng, body, lead):
            for b in range(lead):
                body(None, b)
            with eng.Fori(0, B) as g:
                for c in range(lead, lead + LOOP):
                    body(g, c)
            for b in range(lead + B * LOOP, NB):
                body(None, b)

        @block.sync
        def _(sp):
            for q in range(4):
                sp.dma_start(xs[:, q * QT:(q + 1) * QT, :], x_rows[:, q * QT:(q + 1) * QT, :]).then_inc(x_in[q], 16)
            sp.dma_start(gate_sb[:, :], gate_w).then_inc(cols_in, 16)
            for n, src in enumerate((Wf, Wi, Wh)):
                sp.dma_start(gru_cols[:, n:n + 1], src.rearrange("g o i -> g (o i)")).then_inc(cols_in, 16)
            for n in range(6):
                experts = slice(n % 2 * 4, n % 2 * 4 + 4)
                dst = raw[:, n * RAW:(n + 1) * RAW]
                if n // 2 == W2:
                    sp.dma_start(dst.rearrange("p (e c d) -> p e c d", e=4, c=FC),
                                 w2[experts].rearrange("e (c p) d -> p e c d", p=P)).then_inc(raw_in[n], 16)
                else:
                    sp.dma_start(dst.rearrange("p (e f) -> p e f", e=4),
                                 (w1, w3)[n // 2][experts].rearrange("e p f -> p e f")).then_inc(raw_in[n], 16)
            sp.wait_ge(xn_ready, 4)
            sp.wait_ge(share_step, 3)
            sp.dma_start(xn_rows.rearrange("(t p) d -> p t d", p=P), xn[:, :, :]).then_inc(xn_stored, 16)
            for b in range(NB - LOOP, NB):
                landed(sp, scattered, None, b)
            for k, pieces in ((0, 2), (1, 4)):
                for n in range(pieces):
                    tiles = slice(n * NT // pieces, (n + 1) * NT // pieces)
                    rows = slice(k * T + tiles.start * P, k * T + tiles.stop * P)
                    sp.dma_start(y_back_at[k][:, tiles, :], y_rows[rows, :].rearrange("(t p) d -> p t d", p=P)
                                 ).then_inc(y_back[2 * k + n], 16)
            for q in range(4):
                sp.wait_ge(out_ready, q + 1)
                sp.dma_start(out_rows[:, q * QT:(q + 1) * QT, :], base[:, q * QT:(q + 1) * QT, :]
                             ).then_inc(out_stored, 16)
            sp.wait_ge(out_stored, 64)

        @block.gpsimd
        def _(pool):
            nc.gpsimd.iota(count_up[:, :], [[1, P]], base=0, channel_multiplier=0,
                           allow_small_or_imprecise_dtypes=True).then_inc(count_up_ready, 1)
            nc.gpsimd.memset(ident[:, :], 0.0).then_inc(consts_zero, 1)
            nc.gpsimd.memset(before[:, :], 1.0).then_inc(consts_zero, 1)
            nc.gpsimd.memset(keep_going[:, :, :], 1.0).then_inc(consts_zero, 1)
            nc.gpsimd.memset(ones[:, :], 1.0).then_inc(consts_ready, 1)
            pool.wait_ge(consts_zero, 3)
            nc.gpsimd.affine_select(out=ident[:, :], in_=ident[:, :], compare_op=ALU.not_equal, fill=1.0,
                                    base=0, pattern=[[-1, P]], channel_multiplier=1).then_inc(consts_ready, 1)
            nc.gpsimd.affine_select(out=before[:, :], in_=before[:, :], compare_op=ALU.is_gt, fill=0.0,
                                    base=0, pattern=[[1, P]], channel_multiplier=-1).then_inc(consts_ready, 1)
            nc.gpsimd.memset(keep_going[:, :, 0:1], 0.0).then_inc(consts_ready, 1)
            for tile, pattern, start, per_partition in (
                    (expert_worth[:, :], [[-1, E]], E, 0), (block_edge[:, :], [[P, NT]], 0, 0),
                    (block_no[:, :], [[1, NB]], 0, 0), (token_no1[:, :], [[0, TOP_K], [P, NT]], 1, 1), (dump_row[:, :], [[P, NB]], TOP_K * T + 1, 1)):
                nc.gpsimd.iota(tile, pattern, base=start, channel_multiplier=per_partition,
                               allow_small_or_imprecise_dtypes=True).then_inc(consts_ready, 1)
            pool.wait_ge(cols_in, 64)
            nc.gpsimd.tensor_scalar(minus_cols[:, :], gru_cols[:, :], -1.0, None, ALU.mult).then_inc(minus_ready, 1)
            def low_part(n):
                pool.wait_ge(hi_ready, n + 1)
                at = slice(n * RAW, (n + 1) * RAW)
                nc.gpsimd.tensor_tensor(split[:, LO, at], raw[:, n * RAW:(n + 1) * RAW],
                                        split[:, HI, at].bitcast(F32), ALU.subtract).then_inc(lo_ready, 1)

            for n in range(5):
                low_part(n)

            def gather(b):
                j = b % LOOP
                need(pool, xgT_ps_ready, None, b - LOOP)
                need(pool, slot_share_ready, None, b - LOOP)
                nc.gpsimd.indirect_dma_start(
                    xg[:, j, :], None, xn_rows, bass.IndirectOffsetOnAxis(ap=index[:, b, 0:1], axis=0)
                ).then_inc(gathered[j], 16)

            def scatter(b):
                need(pool, yb_ready, None, b)
                nc.gpsimd.indirect_dma_start(
                    y_rows, bass.IndirectOffsetOnAxis(ap=index[:, b, 1:2], axis=0), yb[:, b % LOOP, :], None
                ).then_inc(scattered[b % LOOP], 16)

            pool.wait_ge(index_ready, 1)
            pool.wait_ge(xn_stored, 16)
            for b in range(LOOP):
                gather(b)
            low_part(5)
            pool.wait_ge(index_ready, 2)
            for b in range(NB):
                if b + LOOP < NB:
                    gather(b + LOOP)
                if b >= 2:
                    scatter(b - 2)
            scatter(NB - 2)
            scatter(NB - 1)

        @block.scalar
        def _(act):
            nc.scalar.preload_act_table(ACT.Sqrt)

            def high_part(n):
                act.wait_ge(raw_in[n], 16)
                nc.scalar.activation(split[:, HI, n * RAW:(n + 1) * RAW], raw[:, n * RAW:(n + 1) * RAW],
                                     ACT.Copy).then_inc(hi_ready, 1)

            def turned(q):
                act.wait_ge(xnT_ps_ready, q + 1)
                nc.scalar.activation(xnT[:, q * QT * P:(q + 1) * QT * P], bank[q][:, :], ACT.Copy
                                     ).then_inc(xnT_ready, 1)

            def std_of(h):
                act.wait_ge(var_ready, h + 1)
                nc.scalar.activation(root[:, h * HT:(h + 1) * HT], var[:, h * HT:(h + 1) * HT], ACT.Sqrt
                                     ).then_inc(root_ready, 1)

            act.wait_ge(count_up_ready, 1)
            nc.scalar.activation(row_no[:, :, :], bcast(count_up[:, :], [[1, P], [0, NSET]]), ACT.Copy
                                 ).then_inc(numbers_ready, 1)
            std_of(0)
            nc.scalar.activation(block_no_of[:, :, :], bcast(count_up[:, :], [[1, NB], [0, NSET]]), ACT.Copy
                                 ).then_inc(numbers_ready, 1)
            turned(0)
            std_of(1)
            turned(1)
            high_part(0)
            for n in range(2, 4):
                turned(n)
            for n in range(1, 4):
                high_part(n)
            nc.scalar.preload_act_table_set("natural_log_exp_and_others")
            act.wait_ge(gap_ready, 1)
            nc.scalar.activation(gap_exp[:, :], gap[:, :], ACT.Exp).then_inc(gap_exp_ready, 1)
            high_part(4)
            act.wait_ge(capped, 8)
            for part in (f_part[:, :], i_part[:, :]):
                nc.scalar.activation(part, part, ACT.Exp).then_inc(exp_ready, 1)
            for n, part in enumerate((f_part[:, :], i_part[:, :])):
                act.wait_ge(exp_ready, n + 1)
                nc.scalar.activation(part, part, ACT.Ln, bias=1.0).then_inc(ln_ready, 1)
            high_part(5)
            act.wait_ge(xnT_ready, 4)
            nc.scalar.activation(hid[:, :], xnT[:, :], ACT.Sigmoid, scale=gru_cols[:, 2:3]).then_inc(hid_ready, 1)
            def update_gate(h):
                act.wait_ge(diff_ready, h + 1)
                nc.scalar.activation(i_part[:, halves[h]], f_part[:, halves[h]], ACT.Sigmoid).then_inc(update_ready, 1)

            def xg_high(g, c):
                need(act, xgT_ps_ready, g, c)
                need(act, up_done, g, c - 2)
                nc.scalar.activation(xg_hi[:, c % 2, :], xgT_ps, ACT.Copy).then_inc(xg_hi_ready, 1)

            def gate(g, c):
                need(act, gate_done, g, c)
                need(act, hb_ready, g, c - 2)
                nc.scalar.activation(silu[:, c % 2, :], gate_ps[c % 2][:, :], ACT.Silu).then_inc(silu_ready, 1)

            def hT_high(g, c):
                need(act, hT_ps_ready, g, c)
                need(act, y_ps_ready, g, c - 2)
                nc.scalar.activation(hT_hi[:, c % 2, :], hT_ps[:, :], ACT.Copy).then_inc(hT_hi_ready, 1)

            def act_block(g, c):
                if g is not None or c < NB - 1:
                    xg_high(g, c + 1)
                gate(g, c)
                if g is not None or c > 0:
                    hT_high(g, c - 1)

            xg_high(None, 0)
            update_gate(0)
            update_gate(1)
            nc.scalar.preload_act_table(ACT.Silu)
            run_blocks(act, act_block, LOOP + 1)
            hT_high(None, NB - 1)

        @block.vector
        def _(dve):
            def stats_of(h):
                for t in range(h * HT, (h + 1) * HT):
                    if t % QT == 0:
                        dve.wait_ge(x_in[t // QT], 16)
                    nc.vector.bn_stats(stats[:, t, :], xs[:, t, :]).then_inc(stats_ready, 1)

            def moments_of(h):
                for t in range(h * HT, (h + 1) * HT):
                    dve.wait_ge(stats_ready, t + 1)
                    nc.vector.bn_aggr(moments[:, t, :], stats[:, t, :]).then_inc(moments_ready, 1)
                dve.wait_ge(moments_ready, (h + 1) * HT)
                nc.vector.tensor_scalar(var[:, h * HT:(h + 1) * HT], moments[:, h * HT:(h + 1) * HT, 1], LN_EPS,
                                        None, ALU.add).then_inc(var_ready, 1)

            def normalised(h):
                at = slice(h * HT, (h + 1) * HT)
                dve.wait_ge(root_ready, h + 1)
                nc.vector.reciprocal(rstd[:, at], root[:, at]).then_inc(rstd_step, 1)
                dve.wait_ge(rstd_step, 4 * h + 1)
                nc.vector.tensor_tensor(newton[:, at], rstd[:, at], rstd[:, at], ALU.mult).then_inc(rstd_step, 1)
                dve.wait_ge(rstd_step, 4 * h + 2)
                nc.vector.scalar_tensor_tensor(out=newton[:, at], in0=var[:, at], scalar=-0.5, in1=newton[:, at],
                                               op0=ALU.mult, op1=ALU.mult).then_inc(rstd_step, 1)
                dve.wait_ge(rstd_step, 4 * h + 3)
                nc.vector.scalar_tensor_tensor(out=rstd[:, at], in0=newton[:, at], scalar=1.5, in1=rstd[:, at],
                                               op0=ALU.add, op1=ALU.mult).then_inc(rstd_step, 1)
                dve.wait_ge(rstd_step, 4 * h + 4)
                for q in (2 * h, 2 * h + 1):
                    for t in range(q * QT, (q + 1) * QT):
                        last = nc.vector.tensor_scalar(xn[:, t, 0:D], xs[:, t, :], moments[:, t, 0:1],
                                                       rstd[:, t:t + 1], ALU.subtract, ALU.mult)
                    last.then_inc(xn_ready, 1)

            stats_of(0)
            moments_of(0)
            stats_of(1)
            normalised(0)
            moments_of(1)
            normalised(1)

            def capped_gates(q):
                dve.wait_ge(xnT_ready, q + 1)
                at = slice(q * QT * P, (q + 1) * QT * P)
                for n, part in enumerate((f_part, i_part)):
                    nc.vector.tensor_scalar(part[:, at], xnT[:, at], minus_cols[:, n:n + 1], GATE_CAP, ALU.mult,
                                            ALU.min).then_inc(capped, 1)

            dve.wait_ge(minus_ready, 1)
            for q in range(3):
                capped_gates(q)

            def flat(tile):
                return tile.rearrange("p t e -> p (t e)")

            dve.wait_ge(consts_ready, NCONST)
            dve.wait_ge(logits_ready, 4)
            nc.vector.tensor_copy(flat(logits[:, 0, :, :]), logits_ps).then_inc(routing_step, 1)
            dve.wait_ge(routing_step, 1)
            for k in range(TOP_K):
                nc.vector.tensor_reduce(top_logit[:, k, :], logits[:, k, :, :], AX.X, ALU.max
                                        ).then_inc(routing_step, 1)
                dve.wait_ge(routing_step, 6 * k + 2)
                nc.vector.tensor_tensor(hits[:, :, :], logits[:, k, :, :], bcast(top_logit[:, k, :], [[1, NT], [0, E]]),
                                        ALU.is_equal).then_inc(routing_step, 1)
                dve.wait_ge(routing_step, 6 * k + 3)
                nc.vector.tensor_tensor(worth[:, :, :], hits[:, :, :], bcast(expert_worth[:, :], [[0, NT], [1, E]]),
                                        ALU.mult).then_inc(routing_step, 1)
                dve.wait_ge(routing_step, 6 * k + 4)
                nc.vector.tensor_reduce(best_worth[:, :], worth[:, :, :], AX.X, ALU.max).then_inc(routing_step, 1)
                dve.wait_ge(routing_step, 6 * k + 5)
                nc.vector.tensor_tensor(is_choice[:, k, :, :], worth[:, :, :],
                                        bcast(best_worth[:, :], [[1, NT], [0, E]]), ALU.is_equal
                                        ).then_inc(routing_step, 1)
                dve.wait_ge(routing_step, 6 * k + 6)
                if k == 0:
                    nc.vector.scalar_tensor_tensor(out=flat(logits[:, 1, :, :]), in0=flat(is_choice[:, 0, :, :]),
                                                   scalar=MASKED, in1=flat(logits[:, 0, :, :]), op0=ALU.mult,
                                                   op1=ALU.add).then_inc(routing_step, 1)
                    dve.wait_ge(routing_step, 7)
            nc.vector.tensor_tensor(chosen[:, :, :], is_choice[:, 0, :, :], is_choice[:, 1, :, :], ALU.add
                                    ).then_inc(chosen_ready, 1)
            nc.vector.tensor_tensor(gap[:, :], top_logit[:, 1, :], top_logit[:, 0, :], ALU.subtract).then_inc(gap_ready, 1)
            capped_gates(3)
            dve.wait_ge(counts_ready, 1)
            nc.vector.tensor_reduce(count[:, :], total_ps.rearrange("p (t e) -> p e t", e=E), AX.X, ALU.add).then_inc(routing_step, 1)
            nc.vector.tensor_copy(run_add[:, :, 1:NT], total_ps.rearrange("p (t e) -> p e t", e=E)[:, :, 0:NT - 1]).then_inc(routing_step, 1)
            dve.wait_ge(routing_step, 13)
            nc.vector.tensor_tensor(over_edge[:, :, :], bcast(count[:, :], [[1, E], [0, NT]]),
                                    bcast(block_edge[:, :], [[0, E], [1, NT]]), ALU.is_gt).then_inc(routing_step, 1)
            dve.wait_ge(routing_step, 15)
            nc.vector.tensor_reduce(blocks[:, :], over_edge[:, :, :], AX.X, ALU.add).then_inc(routing_step, 1)
            dve.wait_ge(routing_step, 16)
            nc.vector.tensor_tensor_scan(blocks_end[:, :], ones[:, 0:E], blocks[:, :], 0.0, ALU.mult, ALU.add).then_inc(routing_step, 1)
            dve.wait_ge(routing_step, 17)
            nc.vector.tensor_tensor(first_block[:, :], blocks_end[:, :], blocks[:, :], ALU.subtract).then_inc(routing_step, 1)
            dve.wait_ge(routing_step, 18)
            nc.vector.tensor_scalar(run_add[:, :, 0], first_block[:, :], float(P), None, ALU.mult).then_inc(routing_step, 1)
            dve.wait_ge(routing_step, 19)
            nc.vector.tensor_tensor_scan(tile_base[:, :, :].rearrange("p e t -> p (e t)"),
                                         keep_going[:, :, :].rearrange("p e t -> p (e t)"),
                                         run_add[:, :, :].rearrange("p e t -> p (e t)"), 0.0, ALU.mult,
                                         ALU.add).then_inc(routing_step, 1)
            dve.wait_ge(routing_step, 20)
            nc.vector.tensor_tensor(slot_of[:, :, :], earlier_ps.rearrange("p (t e) -> p t e", e=E),
                                    tile_base[:, :, :].rearrange("p e t -> p t e"), ALU.add).then_inc(routing_step, 1)
            dve.wait_ge(routing_step, 21)
            nc.vector.tensor_tensor(picked[:, :, :, :].rearrange("p k t e -> p k (t e)"),
                                    is_choice[:, :, :, :].rearrange("p k t e -> p k (t e)"),
                                    bcast(slot_of[:, :, :], [[0, TOP_K], [1, NT * E]]), ALU.mult).then_inc(routing_step, 1)
            dve.wait_ge(routing_step, 22)
            nc.vector.tensor_reduce(slot[:, :].rearrange("p (k t) -> p k t", k=TOP_K), picked[:, :, :, :],
                                    AX.X, ALU.add).then_inc(routing_step, 1)
            dve.wait_ge(routing_step, 23)
            nc.vector.tensor_copy(slot_i[:, :], slot[:, :]).then_inc(routing_step, 1)
            dve.wait_ge(routing_step, 24)
            nc.vector.tensor_scalar(slot_row_i[:, :], slot_i[:, :], P - 1, None, ALU.bitwise_and).then_inc(slot_ready, 1)
            nc.vector.tensor_scalar(slot_block_i[:, :], slot_i[:, :], 7, None, ALU.logical_shift_right).then_inc(slot_ready, 1)
            dve.wait_ge(slot_ready, 2)
            nc.vector.tensor_copy(slot_row[:, :], slot_row_i[:, :]).then_inc(slot_ready, 1)
            nc.vector.tensor_copy(slot_block[:, :], slot_block_i[:, :]).then_inc(slot_ready, 1)
            dve.wait_ge(gap_exp_ready, 1)
            nc.vector.tensor_scalar(gap_sum[:, :], gap_exp[:, :], 1.0, None, ALU.add).then_inc(share_step, 1)
            dve.wait_ge(share_step, 1)
            nc.vector.reciprocal(xn[:, :, D], gap_sum[:, :]).then_inc(share_step, 1)
            dve.wait_ge(share_step, 2)
            nc.vector.tensor_tensor(xn[:, :, D + 1], xn[:, :, D], gap_exp[:, :], ALU.mult).then_inc(share_step, 1)
            dve.wait_ge(slot_ready, 4)
            dve.wait_ge(numbers_ready, 2)
            nc.vector.tensor_tensor(in_row[:, :, :], row_no[:, :, :], bcast(slot_row[:, :], [[0, P], [1, NSET]]),
                                    ALU.is_equal).then_inc(in_row_ready, 1)
            nc.vector.tensor_tensor(in_block[:, :, :], block_no_of[:, :, :],
                                    bcast(slot_block[:, :], [[0, NB], [1, NSET]]), ALU.is_equal
                                    ).then_inc(in_block_ready, 1)
            dve.wait_ge(in_block_ready, 1)
            nc.vector.tensor_tensor(in_block[:, :, :], in_block[:, :, :],
                                    bcast(token_no1[:, :], [[0, NB], [1, NSET]]), ALU.mult
                                    ).then_inc(in_block_ready, 1)
            nc.vector.tensor_tensor(passed[:, :, :], bcast(block_no[0:1, :], [[1, NB], [0, E]]),
                                    bcast(first_block[0:1, :], [[0, NB], [1, E]]), ALU.is_ge).then_inc(routing_step, 1)
            dve.wait_ge(routing_step, 25)
            nc.vector.tensor_reduce(expert_f[:, :], passed[:, :, :], AX.X, ALU.add).then_inc(routing_step, 1)
            dve.wait_ge(routing_step, 26)
            nc.vector.tensor_scalar(expert_at[:, :], expert_f[:, :], float(F), -float(F), ALU.mult, ALU.add).then_inc(expert_ready, 1)
            def softplus(h):
                for n, part in enumerate((f_part, i_part)):
                    dve.wait_ge(ln_ready, n + 1)
                    nc.vector.scalar_tensor_tensor(out=part[:, halves[h]], in0=xnT[:, halves[h]],
                                                   scalar=minus_cols[:, n:n + 1], in1=part[:, halves[h]],
                                                   op0=ALU.mult, op1=ALU.max).then_inc(softplus_ready, 1)

            def difference(h):
                dve.wait_ge(softplus_ready, 2 * h + 2)
                nc.vector.tensor_tensor(f_part[:, halves[h]], f_part[:, halves[h]], i_part[:, halves[h]],
                                        ALU.subtract).then_inc(diff_ready, 1)

            softplus(0)
            dve.wait_ge(inverse_ready, 1)
            nc.vector.tensor_copy(inv1[:, :, :].rearrange("p k b -> p (k b)"), inverse_ps).then_inc(routing_step, 1)
            dve.wait_ge(routing_step, 27)
            nc.vector.tensor_tensor(any1[:, :], inv1[:, 0, :], inv1[:, 1, :], ALU.add).then_inc(routing_step, 1)
            nc.vector.tensor_scalar(is_first[:, :], inv1[:, 1, :], 0.0, None, ALU.is_equal)
            nc.vector.tensor_scalar(second[:, :], inv1[:, 1, :], 0.0, float(T), ALU.is_gt, ALU.mult).then_inc(routing_step, 1)
            dve.wait_ge(routing_step, 29)
            nc.vector.tensor_scalar(index[:, :, 0], any1[:, :], -1.0, 0.0, ALU.add, ALU.max).then_inc(index_ready, 1)
            nc.vector.scalar_tensor_tensor(out=empty[:, :], in0=any1[:, :], scalar=0.0, in1=dump_row[:, :],
                                           op0=ALU.is_equal, op1=ALU.mult).then_inc(routing_step, 1)
            nc.vector.scalar_tensor_tensor(out=dest_a[:, :], in0=any1[:, :], scalar=-1.0, in1=second[:, :],
                                           op0=ALU.add, op1=ALU.add).then_inc(routing_step, 1)
            dve.wait_ge(routing_step, 31)
            nc.vector.tensor_tensor(index[:, :, 1], dest_a[:, :], empty[:, :], ALU.add).then_inc(index_ready, 1)

            difference(0)
            softplus(1)
            difference(1)

            def share_of(g, c):
                landed(dve, gathered, g, c)
                need(dve, hb_ready, g, c - 2)
                nc.vector.scalar_tensor_tensor(out=slot_share[:, c % 2:c % 2 + 1], in0=xg[:, c % LOOP, D:D + 1],
                                               scalar=is_first[:, bass.ds(number(g, c), 1)],
                                               in1=xg[:, c % LOOP, D + 1:D + 2], op0=ALU.mult, op1=ALU.max
                                               ).then_inc(slot_share_ready, 1)

            def xg_low(g, c):
                need(dve, xg_hi_ready, g, c)
                need(dve, up_done, g, c - 2)
                nc.vector.tensor_tensor(xg_lo[:, c % 2, :], xgT_ps, xg_hi[:, c % 2, :].bitcast(F32), ALU.subtract
                                        ).then_inc(xg_lo_ready, 1)

            def gated(g, c):
                need(dve, up_done, g, c)
                need(dve, silu_ready, g, c)
                need(dve, hT_ps_ready, g, c - 2)
                need(dve, slot_share_ready, g, c)
                nc.vector.scalar_tensor_tensor(out=hb[:, c % 2, :], in0=silu[:, c % 2, :],
                                               scalar=slot_share[:, c % 2:c % 2 + 1], in1=up_ps[c % 2][:, :],
                                               op0=ALU.mult, op1=ALU.mult).then_inc(hb_ready, 1)

            def hT_low(g, c):
                need(dve, hT_hi_ready, g, c)
                need(dve, y_ps_ready, g, c - 2)
                nc.vector.tensor_tensor(hT_lo[:, c % 2, :], hT_ps[:, :], hT_hi[:, c % 2, :].bitcast(F32), ALU.subtract
                                        ).then_inc(hT_lo_ready, 1)

            def result(g, c):
                need(dve, y_ps_ready, g, c)
                landed(dve, scattered, g, c - LOOP)
                nc.vector.tensor_reduce(yb[:, c % LOOP, :], y_ps.rearrange("p (n d) -> p d n", n=2), AX.X, ALU.add
                                        ).then_inc(yb_ready, 1)

            def gate_parts(r):
                dve.wait_ge(hid_ready, 1)
                dve.wait_ge(update_ready, 2)
                seq = bass.ds(r * S, S)
                nc.vector.tensor_scalar(relu_seq[:, :], xnT[:, seq], gru_cols[:, 2:3], 0.0, ALU.mult, ALU.max
                                        ).then_inc(seq_step, 1)
                nc.vector.tensor_scalar(keep_seq[:, :], i_part[:, seq], -1.0 - EPS, 1.0 + EPS, ALU.mult, ALU.add
                                        ).then_inc(seq_step, 1)
                dve.wait_ge(seq_step, r * 4 + 1)
                nc.vector.scalar_tensor_tensor(out=value_seq[:, :], in0=hid[:, seq], scalar=0.5 + EPS,
                                               in1=relu_seq[:, :], op0=ALU.min, op1=ALU.add).then_inc(seq_step, 1)

            def scanned(r):
                dve.wait_ge(seq_step, r * 4 + 3)
                nc.vector.tensor_tensor(value_seq[:, :], value_seq[:, :], i_part[:, bass.ds(r * S, S)], ALU.mult
                                        ).then_inc(seq_step, 1)
                dve.wait_ge(seq_step, r * 4 + 4)
                nc.vector.tensor_tensor_scan(h_seq[:, :], keep_seq[:, :], value_seq[:, :], 0.0, ALU.mult, ALU.add
                                             ).then_inc(h_seq_ready, 1)

            def added(r):
                dve.wait_ge(h_ps_ready, r + 1)
                tiles = bass.ds(r * (S // P), S // P)
                nc.vector.tensor_tensor(base[:, tiles, :], h_ps.rearrange("p (t d) -> p t d", d=D), xs[:, tiles, :],
                                        ALU.add).then_inc(base_ready, 1)

            def dve_block(g, c):
                if g is not None or c < NB - 1:
                    share_of(g, c + 1)
                    xg_low(g, c + 1)
                gated(g, c)
                if g is not None or c > 0:
                    hT_low(g, c - 1)
                if g is not None or c > 1:
                    result(g, c - 2)
                if g is not None and c % LOOP == 2:
                    gate_parts(g)
                if g is not None and c % LOOP == 3:
                    scanned(g)
                if g is not None and c % LOOP == 1:
                    added(g)

            share_of(None, 0)
            xg_low(None, 0)
            run_blocks(dve, dve_block, LOOP + 2)
            hT_low(None, NB - 1)
            result(None, NB - 2)
            result(None, NB - 1)

            dve.wait_ge(base_ready, B)
            for k, pieces in ((0, 2), (1, 4)):
                for n in range(pieces):
                    tiles = slice(n * NT // pieces, (n + 1) * NT // pieces)
                    dve.wait_ge(y_back[2 * k + n], 16)
                    if k == 1:
                        dve.wait_ge(first_added, n // 2 + 1)
                    nc.vector.tensor_tensor(base[:, tiles, :], base[:, tiles, :], y_back_at[k][:, tiles, :], ALU.add
                                            ).then_inc(out_ready if k == 1 else first_added, 1)

        @block.tensor
        def _(pe):
            pe.wait_ge(consts_ready, NCONST)

            def stay_warm(count, idle_bank=7):
                for _ in range(count):
                    nc.tensor.matmul(bank[idle_bank][:, 3 * P:], ones[:, :], before[:, :], start=True, stop=True)

            def logits_of(q):
                pe.wait_ge(cols_in, 64)
                pe.wait_ge(xnT_ready, q + 1)
                for t in range(q * QT, (q + 1) * QT):
                    last = nc.tensor.matmul(logits_ps[:, t * E:(t + 1) * E], xnT[:, t * P:(t + 1) * P], gate_sb[:, :],
                                            start=True, stop=True)
                last.then_inc(logits_ready, 1)

            stay_warm(WARM_START)
            def turn_xn(q):
                pe.wait_ge(xn_ready, q + 1)
                for t in range(q * QT, (q + 1) * QT):
                    last = nc.tensor.transpose(bank[q][:, (t % QT) * P:(t % QT + 1) * P], xn[:, t, 0:D], ident[:, :])
                last.then_inc(xnT_ps_ready, 1)

            for q in range(4):
                turn_xn(q)
                if q % 2 == 1:
                    stay_warm(WARM_TURN)
                    logits_of(q - 1)
                    stay_warm(WARM_TURN)
                    logits_of(q)
                    stay_warm(WARM_TURN)
            pe.wait_ge(chosen_ready, 1)
            picks = chosen[:, :, :].rearrange("p t e -> p (t e)")
            nc.tensor.matmul(earlier_ps, before[:, :], picks, start=True, stop=True)
            nc.tensor.matmul(total_ps, ones[:, :], picks, start=True, stop=True).then_inc(counts_ready, 1)
            stay_warm(WARM_INVERSE)
            pe.wait_ge(in_row_ready, 1)
            pe.wait_ge(in_block_ready, 2)
            for k in range(TOP_K):
                for t in range(NT):
                    last = nc.tensor.matmul(inverse_ps[:, k * NB:(k + 1) * NB], in_row[:, :, k * NT + t],
                                            in_block[:, :, k * NT + t], start=(t == 0), stop=(t == NT - 1))
            last.then_inc(inverse_ready, 1)
            stay_warm(WARM_BLOCKS, 6)

            def weights_of(name, first, count):
                regs = [pe.alloc_register(f"{name}_at{n}") for n in range(count)]
                pe.reg_load(regs, expert_at[0:1, bass.ds(first, count)])
                return [pe.snap(reg, donate=True, min_val=0, max_val=(E - 1) * F) for reg in regs]

            def weights(part, at, width):
                return split[:, part, bass.ds(at, width)]

            def product(out_ps, j, at):
                nc.tensor.matmul(out_ps, xg_hi[:, j, :], weights(HI, at, F), start=True, stop=False)
                nc.tensor.matmul(out_ps, xg_hi[:, j, :], weights(LO, at, F), start=False, stop=False)
                return nc.tensor.matmul(out_ps, xg_lo[:, j, :], weights(HI, at, F), start=False, stop=True)

            def turn_x(g, c):
                landed(pe, gathered, g, c)
                need(pe, xg_lo_ready, g, c - 1)
                nc.tensor.transpose(xgT_ps, xg[:, c % LOOP, 0:D], ident[:, :]).then_inc(xgT_ps_ready, 1)

            def up(g, c, at):
                j = c % 2
                need(pe, xg_lo_ready, g, c)
                need(pe, silu_ready, g, c - 2)
                need(pe, hb_ready, g, c - 2)
                product(gate_ps[j][:, :], j, at + W1 * E * F).then_inc(gate_done, 1)
                product(up_ps[j][:, :], j, at + W3 * E * F).then_inc(up_done, 1)

            def turn_h(g, c):
                need(pe, hb_ready, g, c)
                need(pe, hT_lo_ready, g, c - 1)
                for f in range(FC):
                    last = nc.tensor.transpose(hT_ps[:, f * P:(f + 1) * P], hb[:, c % 2, f * P:(f + 1) * P],
                                               ident[:, :])
                last.then_inc(hT_ps_ready, 1)

            def down(g, c, at):
                j = c % 2
                need(pe, hT_lo_ready, g, c)
                need(pe, yb_ready, g, c - 1)
                for f in range(FC):
                    rows = slice(f * P, (f + 1) * P)
                    w_at = at + (W2 * E * F + f * D)
                    nc.tensor.matmul(y_ps.rearrange("p (n d) -> p n d", n=2), hT_hi[:, j, rows],
                                     split[:, :, bass.ds(w_at, D)], start=(f == 0), stop=False)
                    last = nc.tensor.matmul(y_ps[:, P:2 * P], hT_lo[:, j, rows], weights(HI, w_at, D),
                                            start=False, stop=(f == FC - 1))
                last.then_inc(y_ps_ready, 1)

            def turn_seq(r):
                pe.wait_ge(h_seq_ready, r + 1)
                for t in range(S // P):
                    last = nc.tensor.transpose(h_ps[:, t * P:(t + 1) * P], h_seq[:, t * P:(t + 1) * P], ident[:, :])
                last.then_inc(h_ps_ready, 1)

            def pe_block(g, c, weights_at):
                if g is not None or c > 1:
                    turn_h(g, c - 2)
                if g is None and c == 3:
                    pe.wait_ge(lo_ready, 6)
                if g is not None or c > 2:
                    down(g, c - 3, weights_at[-4])
                if g is not None and c % LOOP == 1:
                    turn_seq(g)
                if g is not None or c < NB - 1:
                    turn_x(g, c + 1)
                up(g, c, weights_at[-1])

            pe.wait_ge(expert_ready, 1)
            pe.wait_ge(index_ready, 1)
            pe.wait_ge(lo_ready, 4)
            lead = LOOP + 2
            weights_at = weights_of("first", 0, lead)
            turn_x(None, 0)
            for c in range(lead):
                pe_block(None, c, weights_at[:c + 1])
            with pe.Fori(0, B) as g:
                weights_at = weights_of("turn", g * LOOP + (lead - 3), LOOP + 3)
                for c in range(lead, lead + LOOP):
                    pe_block(g, c, weights_at[:c - lead + 4])
            after = lead + LOOP * B
            weights_at = weights_of("last", after - 3, NB - after + 3)
            for c in range(after, NB):
                pe_block(None, c, weights_at[:c - after + 4])
            turn_h(None, NB - 2)
            down(None, NB - 3, weights_at[-3])
            turn_h(None, NB - 1)
            down(None, NB - 2, weights_at[-2])
            down(None, NB - 1, weights_at[-1])


_INS = ['L0_attn_x_t', 'L0_attn_Wf', 'L0_attn_Wi', 'L0_attn_Wh', 'L0_ffn_gate_w', 'L0_ffn_w1', 'L0_ffn_w3', 'L0_ffn_w2']
_OUTS = [((8, 256, 128), 'float32')]


def kernel(**inputs):
    import numpy as _np
    import concourse.bacc as _bacc
    from concourse import mybir as _mybir
    from concourse.bass_utils import run_bass_kernel_spmd as _run

    nc = _bacc.Bacc("TRN2", target_bir_lowering=False, num_devices=1)
    arrays, args = {}, []
    for name in _INS:
        a = _np.ascontiguousarray(inputs[name])
        arrays[f"in_{name}_dram"] = a
        args.append(nc.dram_tensor(f"in_{name}_dram", a.shape, _mybir.dt.from_np(a.dtype), kind="ExternalInput").ap())
    for i, (shape, dtype) in enumerate(_OUTS):
        dt = _mybir.dt.from_np(_np.dtype(dtype))
        args.append(nc.dram_tensor(f"out_{i}_dram", shape, dt, kind="ExternalOutput").ap())
    mixed_layer(nc, *args)
    r = _run(nc, [arrays], core_ids=[0])
    got = tuple(r.results[0][f"out_{i}_dram"] for i in range(len(_OUTS)))
    return got[0]
```
